# Optimizing a Trainium2 kernel written in Bass

```python
import numpy as np
import jax
import jax.numpy as jnp

def _softmax(x, axis=-1):
    return jax.nn.softmax(x, axis=axis)
def _gelu(x):
    return jax.nn.gelu(x, approximate=True)
def _silu(x):
    return jax.nn.silu(x)
def _sigmoid(x):
    return jax.nn.sigmoid(x)
def _layernorm(x, axis=-1, eps=1e-5):
    m = jnp.mean(x, axis=axis, keepdims=True)
    v = jnp.var(x, axis=axis, keepdims=True)
    return (x - m) / jnp.sqrt(v + eps)
def _scatter_add(tgt, idx, src, axis=0):
    return tgt.at[idx].add(src)
def _segment_sum(src, seg, n):
    return jax.ops.segment_sum(src, seg, n)

kernel_name = 'mk_conv_seq_d2_conv_nchw64_06bdce'

def setup_inputs(seed: int = 0):
    np.random.seed(seed)
    _w = jnp.asarray
    def _rec_inputs():
        import jax
        import jax.numpy as jnp
        _gk = jax.random.key(seed)
        x = -0.0002928 + 1 * jax.random.normal(jax.random.fold_in(_gk, 1), (16, 64, 64, 64), jnp.float32)
        return x
    x = _rec_inputs()
    def _L0_conv_setup():
        import jax, jax.numpy as jnp
        import numpy as np
        from jax import lax
        DN = ('NCHW', 'OIHW', 'NCHW')

        def _conv(x, w, pad):
            return lax.conv_general_dilated(x, w, (1, 1), [(pad, pad), (pad, pad)], dimension_numbers=DN)

        def _bn(x, gamma, beta, mean, var, eps=1e-05):
            inv = gamma * lax.rsqrt(var + eps)
            return x * inv[None, :, None, None] + (beta - mean * inv)[None, :, None, None]

        def _unfold(x, K, pad):
            B, C, H, W = x.shape
            p = lax.conv_general_dilated_patches(x, (K, K), (1, 1), [(pad, pad), (pad, pad)], dimension_numbers=DN)
            return p.reshape(B, C, K * K, H, W)
        key = jax.random.key(seed)
        ks = jax.random.split(key, 16)
        B, C, H, W, K = (16, 64, 64, 64, 3)
        d = {'x': jax.random.normal(ks[0], (B, C, H, W), jnp.float32), 'wq': jax.random.normal(ks[1], (C, C, 1, 1), jnp.float32) * 0.1, 'wk': jax.random.normal(ks[2], (C, C, K, K), jnp.float32) * 0.05, 'wv': jax.random.normal(ks[3], (C, C, 1, 1), jnp.float32) * 0.1, 'pos_h': jax.random.normal(ks[4], (C, K, 1), jnp.float32), 'pos_w': jax.random.normal(ks[5], (C, 1, K), jnp.float32)}
        for i, nm in enumerate(['q', 'k', 'v', 'o']):
            d[nm + '_gamma'] = jnp.ones((C,), jnp.float32)
            d[nm + '_beta'] = jnp.zeros((C,), jnp.float32)
            d[nm + '_mean'] = jax.random.normal(ks[6 + i], (C,), jnp.float32) * 0.1
            d[nm + '_var'] = jax.random.uniform(ks[10 + i], (C,), jnp.float32, 0.5, 1.5)
        return d
    _L0_conv_all = _L0_conv_setup()
    _L0_conv_in = {k: v for k, v in _L0_conv_all.items() if k in ('wq', 'q_gamma', 'q_beta', 'q_mean', 'q_var', 'wk', 'k_gamma', 'k_beta', 'k_mean', 'k_var', 'wv', 'v_gamma', 'v_beta', 'v_mean', 'v_var', 'pos_h', 'pos_w', 'o_gamma', 'o_beta', 'o_mean', 'o_var', )}
    del _L0_conv_all

    def _L1_conv_setup():
        import jax, jax.numpy as jnp
        import numpy as np

        def _proj(x, Wc, bc):
            b, c, h, w = x.shape
            y = jnp.einsum('oc,bchw->bohw', Wc, x) + bc[None, :, None, None]
            return y.reshape(b, Wc.shape[0], h * w)
        key = jax.random.key(seed)
        ks = jax.random.split(key, 5)
        B, C, H, W = (8, 64, 64, 64)
        Ci = 32
        s = 1.0 / np.sqrt(C)
        return {'x': jax.random.normal(ks[0], (B, C, H, W), jnp.float32), 'Wg': jax.random.normal(ks[1], (Ci, C), jnp.float32) * s, 'bg': jnp.zeros((Ci,), jnp.float32), 'Wt': jax.random.normal(ks[2], (Ci, C), jnp.float32) * s, 'bt': jnp.zeros((Ci,), jnp.float32), 'Wp': jax.random.normal(ks[3], (Ci, C), jnp.float32) * s, 'bp': jnp.zeros((Ci,), jnp.float32), 'Ww': jax.random.normal(ks[4], (C, Ci), jnp.float32) * (1.0 / np.sqrt(Ci)), 'bw': jnp.zeros((C,), jnp.float32)}
    _L1_conv_all = _L1_conv_setup()
    _L1_conv_in = {k: v for k, v in _L1_conv_all.items() if k in ('Wg', 'bg', 'Wt', 'bt', 'Wp', 'bp', 'Ww', 'bw', )}
    del _L1_conv_all

    return {
        "x": x,
        "L0_conv_wq": _L0_conv_in["wq"],
        "L0_conv_q_gamma": _L0_conv_in["q_gamma"],
        "L0_conv_q_beta": _L0_conv_in["q_beta"],
        "L0_conv_q_mean": _L0_conv_in["q_mean"],
        "L0_conv_q_var": _L0_conv_in["q_var"],
        "L0_conv_wk": _L0_conv_in["wk"],
        "L0_conv_k_gamma": _L0_conv_in["k_gamma"],
        "L0_conv_k_beta": _L0_conv_in["k_beta"],
        "L0_conv_k_mean": _L0_conv_in["k_mean"],
        "L0_conv_k_var": _L0_conv_in["k_var"],
        "L0_conv_wv": _L0_conv_in["wv"],
        "L0_conv_v_gamma": _L0_conv_in["v_gamma"],
        "L0_conv_v_beta": _L0_conv_in["v_beta"],
        "L0_conv_v_mean": _L0_conv_in["v_mean"],
        "L0_conv_v_var": _L0_conv_in["v_var"],
        "L0_conv_pos_h": _L0_conv_in["pos_h"],
        "L0_conv_pos_w": _L0_conv_in["pos_w"],
        "L0_conv_o_gamma": _L0_conv_in["o_gamma"],
        "L0_conv_o_beta": _L0_conv_in["o_beta"],
        "L0_conv_o_mean": _L0_conv_in["o_mean"],
        "L0_conv_o_var": _L0_conv_in["o_var"],
        "L1_conv_Wg": _L1_conv_in["Wg"],
        "L1_conv_bg": _L1_conv_in["bg"],
        "L1_conv_Wt": _L1_conv_in["Wt"],
        "L1_conv_bt": _L1_conv_in["bt"],
        "L1_conv_Wp": _L1_conv_in["Wp"],
        "L1_conv_bp": _L1_conv_in["bp"],
        "L1_conv_Ww": _L1_conv_in["Ww"],
        "L1_conv_bw": _L1_conv_in["bw"],
    }

def reference(x, L0_conv_wq, L0_conv_q_gamma, L0_conv_q_beta, L0_conv_q_mean, L0_conv_q_var, L0_conv_wk, L0_conv_k_gamma, L0_conv_k_beta, L0_conv_k_mean, L0_conv_k_var, L0_conv_wv, L0_conv_v_gamma, L0_conv_v_beta, L0_conv_v_mean, L0_conv_v_var, L0_conv_pos_h, L0_conv_pos_w, L0_conv_o_gamma, L0_conv_o_beta, L0_conv_o_mean, L0_conv_o_var, L1_conv_Wg, L1_conv_bg, L1_conv_Wt, L1_conv_bt, L1_conv_Wp, L1_conv_bp, L1_conv_Ww, L1_conv_bw):
    import jax
    import jax.numpy as jnp
    def _L0_conv_ref(x, wq, q_gamma, q_beta, q_mean, q_var, wk, k_gamma, k_beta, k_mean, k_var, wv, v_gamma, v_beta, v_mean, v_var, pos_h, pos_w, o_gamma, o_beta, o_mean, o_var):
        import jax, jax.numpy as jnp
        import numpy as np
        from jax import lax
        DN = ('NCHW', 'OIHW', 'NCHW')

        def _conv(x, w, pad):
            return lax.conv_general_dilated(x, w, (1, 1), [(pad, pad), (pad, pad)], dimension_numbers=DN)

        def _bn(x, gamma, beta, mean, var, eps=1e-05):
            inv = gamma * lax.rsqrt(var + eps)
            return x * inv[None, :, None, None] + (beta - mean * inv)[None, :, None, None]

        def _unfold(x, K, pad):
            B, C, H, W = x.shape
            p = lax.conv_general_dilated_patches(x, (K, K), (1, 1), [(pad, pad), (pad, pad)], dimension_numbers=DN)
            return p.reshape(B, C, K * K, H, W)
        B, C, H, W = x.shape
        K = pos_h.shape[1]
        heads = C // 8
        cph = C // heads
        q = jax.nn.relu(_bn(_conv(x, wq, 0), q_gamma, q_beta, q_mean, q_var))
        k = jax.nn.relu(_bn(_conv(x, wk, K // 2), k_gamma, k_beta, k_mean, k_var))
        v = _bn(_conv(x, wv, 0), v_gamma, v_beta, v_mean, v_var)
        unfold_k = _unfold(k, K, K // 2)
        pos = (pos_h + pos_w).reshape(1, C, K * K, 1, 1)
        kp = (unfold_k + pos).reshape(B, heads, cph, K * K, H, W)
        qh = q.reshape(B, heads, cph, 1, H, W)
        attn = (qh * kp).sum(axis=2)
        attn = jax.nn.softmax(attn, axis=2)
        uv = _unfold(v, K, (K - 1) // 2).reshape(B, heads, cph, K * K, H, W)
        out = (attn[:, :, None] * uv).sum(axis=3).reshape(B, C, H, W)
        out = jax.nn.relu(_bn(out, o_gamma, o_beta, o_mean, o_var))
        return out

    def _L1_conv_ref(x, Wg, bg, Wt, bt, Wp, bp, Ww, bw):
        import jax, jax.numpy as jnp
        import numpy as np

        def _proj(x, Wc, bc):
            b, c, h, w = x.shape
            y = jnp.einsum('oc,bchw->bohw', Wc, x) + bc[None, :, None, None]
            return y.reshape(b, Wc.shape[0], h * w)
        b, c, h, w = x.shape
        g_x = _proj(x, Wg, bg).transpose(0, 2, 1)
        theta_x = _proj(x, Wt, bt).transpose(0, 2, 1)
        phi_x = _proj(x, Wp, bp)
        f = jnp.einsum('bnd,bdm->bnm', theta_x, phi_x)
        f_div_C = jax.nn.softmax(f, axis=-1)
        y = jnp.einsum('bnm,bmd->bnd', f_div_C, g_x)
        y = y.transpose(0, 2, 1).reshape(b, Wg.shape[0], h, w)
        W_y = jnp.einsum('od,bdhw->bohw', Ww, y) + bw[None, :, None, None]
        return W_y + x

    def _gn(v, G=32, eps=1e-5):
        B_, C_, H_, W_ = v.shape
        g = v.reshape(B_, G, C_ // G, H_, W_)
        m = jnp.mean(g, axis=(2, 3, 4), keepdims=True)
        s = jnp.var(g, axis=(2, 3, 4), keepdims=True)
        return ((g - m) / jnp.sqrt(s + eps)).reshape(v.shape)

    def _ln_c(v, eps=1e-6):
        m = jnp.mean(v, axis=1, keepdims=True)
        s = jnp.var(v, axis=1, keepdims=True)
        return (v - m) / jnp.sqrt(s + eps)

    def _ln_t(v, eps=1e-5):
        m = jnp.mean(v, axis=-1, keepdims=True)
        s = jnp.var(v, axis=-1, keepdims=True)
        return (v - m) / jnp.sqrt(s + eps)

    def _to_tokens(v):
        B_, C_, H_, W_ = v.shape
        return v.reshape(B_, C_, H_ * W_).transpose(0, 2, 1)
    def _from_tokens(t, like):
        B_, C_, H_, W_ = like.shape
        return t.transpose(0, 2, 1).reshape(B_, C_, H_, W_)

    x = _L0_conv_ref(x, L0_conv_wq, L0_conv_q_gamma, L0_conv_q_beta, L0_conv_q_mean, L0_conv_q_var, L0_conv_wk, L0_conv_k_gamma, L0_conv_k_beta, L0_conv_k_mean, L0_conv_k_var, L0_conv_wv, L0_conv_v_gamma, L0_conv_v_beta, L0_conv_v_mean, L0_conv_v_var, L0_conv_pos_h, L0_conv_pos_w, L0_conv_o_gamma, L0_conv_o_beta, L0_conv_o_mean, L0_conv_o_var)
    x = _L1_conv_ref(x, L1_conv_Wg, L1_conv_bg, L1_conv_Wt, L1_conv_bt, L1_conv_Wp, L1_conv_bp, L1_conv_Ww, L1_conv_bw)
    return x


_drawn_inputs = setup_inputs


def setup_inputs(seed=0):
    import zlib

    import numpy as np

    out = dict(_drawn_inputs(seed))
    spreads = {'L0_conv_q_gamma': (1.0, 0.2),
     'L0_conv_q_beta': (0.0, 0.1),
     'L0_conv_k_gamma': (1.0, 0.2),
     'L0_conv_k_beta': (0.0, 0.302),
     'L0_conv_v_gamma': (1.0, 0.2),
     'L0_conv_v_beta': (0.0, 0.1),
     'L0_conv_o_gamma': (1.0, 0.2),
     'L0_conv_o_beta': (0.0, 0.1),
     'L1_conv_bg': (0.0, 0.1),
     'L1_conv_bt': (0.0, 0.418),
     'L1_conv_bp': (0.0, 0.8),
     'L1_conv_bw': (0.0, 0.1)}
    factors = {}
    for name, (base, spread) in spreads.items():
        noise = np.random.default_rng([zlib.crc32(name.encode()), seed]).standard_normal(out[name].shape)
        drawn = base * np.exp(spread * noise) if base else spread * noise
        out[name] = jnp.asarray(drawn.astype(out[name].dtype))
    for name, factor in factors.items():
        out[name] = (out[name] * factor).astype(out[name].dtype)
    return out
```

```python
from contextlib import ExitStack

import numpy as np

import concourse.bass as bass
from concourse import mybir

F32 = mybir.dt.float32
F32R = mybir.dt.float32r
ALU = mybir.AluOpType
ACT = mybir.ActivationFunctionType
AX_X = mybir.AxisListType.X

B, C, H, W = 16, 64, 64, 64
HW = H * W
K = 3
TAPS = K * K
HEADS = C // 8
CPH = C // HEADS
CI = 32
EPS = 1e-5
P = 128
PAIRS = B // 2
HP, WP = H + 2, W + 2
CH = 512
CHUNKS = HW // CH
CR = CH // W
QT = 1024
QUARTERS = HW // QT
QR = QT // W
GP = QT // 8
MT = HW // P
STEPS = MT // 2


def layer0_attention(nc, x, consts, x1):
    with ExitStack() as ctx:
        def sb(name, shape, dt=F32):
            return ctx.enter_context(nc.sbuf_tensor(name, shape, dt))

        def sem(name):
            return ctx.enter_context(nc.semaphore(name))

        wk = sb("wk", [P, 2 * K, C])
        wq = sb("wq", [P, C])
        wv = sb("wv", [P, C])
        headsum = sb("headsum", [P, 2, 32])
        sel_f = sb("sel_f", [P, 8, P])
        sel = sb("sel", [P, 8, P], F32R)
        bn = sb("bn", [P, 4, 4])
        posh = sb("posh", [P, K])
        posw = sb("posw", [P, K])
        pos = sb("pos", [P, K, K])
        veps = sb("veps", [P, 4])
        root = sb("root", [P, 4])
        quot = sb("quot", [P, 4])
        root2 = sb("root2", [P, 4])
        rinv = sb("rinv", [P, 4])
        inv = sb("inv", [P, 4])
        mi = sb("mi", [P, 4])
        shift = sb("shift", [P, 4])
        spare = sb("spare", [P, 8])
        xp = sb("xp", [P, 2, HP, WP])
        kp = sb("kp", [P, HP, WP])
        vp = sb("vp", [P, HP, WP])
        q = sb("q", [P, HW])
        prod = sb("prod", [P, 3, QT])
        lmax = sb("lmax", [P, GP])
        lsub = sb("lsub", [P, TAPS, GP])
        attn = sb("attn", [P, TAPS, GP])
        lsum = sb("lsum", [P, GP])
        lrcp = sb("lrcp", [P, GP])
        attn_hi = sb("attn_hi", [P, TAPS, GP], F32R)
        attn_lo = sb("attn_lo", [P, TAPS, GP], F32R)
        av = sb("av", [P, 3, CH])
        acc = sb("acc", [P, 2, CH])
        xo = sb("xo", [P, 2, CH])
        ps = ctx.enter_context(nc.psum_tensor("psa", [P, 8, CH], F32))

        const_in = sem("const_in")
        zeroed = sem("zeroed")
        bn_step = sem("bn_step")
        root_ready = sem("root_ready")
        sel_ready = sem("sel_ready")
        x_in = sem("x_in")
        conv_done = sem("conv_done")
        conv_free = sem("conv_free")
        prod_ready = sem("prod_ready")
        prod_free = sem("prod_free")
        max_ready = sem("max_ready")
        sub_ready = sem("sub_ready")
        exp_ready = sem("exp_ready")
        sum_ready = sem("sum_ready")
        rcp_ready = sem("rcp_ready")
        attn_ready = sem("attn_ready")
        hi_ready = sem("hi_ready")
        lo_ready = sem("lo_ready")
        spread_done = sem("spread_done")
        av_ready = sem("av_ready")
        av_free = sem("av_free")
        xo_ready = sem("xo_ready")
        xo_free = [sem("xo_free0"), sem("xo_free1")]

        x_pairs = x.rearrange("(p i) c h w -> c p i h w", i=2)
        x1_rows = x1.rearrange("(p i) c n -> (i c) p n", i=2)
        loads = [(wk, "wk"), (wq, "wq"), (wv, "wv"), (headsum, "headsum"), (sel_f, "sel"),
                 (bn, "bn"), (posh, "pos_h"), (posw, "pos_w")]

        block = ctx.enter_context(nc.Block())

        @block.sync
        def _(sp):
            for dst, name in loads:
                sp.dma_start(dst[:], consts[name]).then_inc(const_in, 16)

            def load_pair(pair):
                for i in range(2):
                    src = x_pairs[:, bass.ds(pair, 1), i]
                    sp.dma_start(xp[0:C, i:i + 1, 1:H + 1, 1:W + 1], src).then_inc(x_in, 16)
                    sp.dma_start(xp[C:P, i:i + 1, 0:H, 1:W + 1], src).then_inc(x_in, 16)

            def store_pair(pair):
                with sp.Fori(0, CHUNKS // 2) as cc:
                    for par in range(2):
                        n = pair * CHUNKS + cc * 2 + par
                        sp.wait_ge(xo_ready, 2 + n + 1)
                        sp.dma_start(x1_rows[:, bass.ds(pair, 1), bass.ds((cc * 2 + par) * CH, CH)],
                                     xo[:, par:par + 1, :]).then_inc(xo_free[par], 16)

            sp.wait_ge(zeroed, 3)
            load_pair(0)
            with sp.Fori(0, PAIRS - 1) as pair:
                sp.wait_ge(conv_done, 3 * CHUNKS * (pair + 1))
                load_pair(pair + 1)
                store_pair(pair)
            store_pair(PAIRS - 1)
            for par in range(2):
                sp.wait_ge(xo_free[par], 16 + 16 * B * CHUNKS // 4)

        @block.vector
        def _(dve):
            nc.vector.memset(xp[:], 0.0).then_inc(zeroed, 1)
            nc.vector.memset(kp[:], 0.0).then_inc(zeroed, 1)
            nc.vector.memset(vp[:], 0.0).then_inc(zeroed, 1)
            dve.wait_ge(const_in, 16 * len(loads))
            nc.vector.tensor_copy(sel[:], sel_f[:]).then_inc(sel_ready, 1)
            nc.vector.tensor_scalar(veps[:], bn[:, 3, :], EPS, None, ALU.add).then_inc(bn_step, 1)
            dve.wait_ge(root_ready, 1)
            nc.vector.reciprocal(quot[:], root[:]).then_inc(bn_step, 1)
            dve.wait_ge(bn_step, 2)
            nc.vector.tensor_tensor(quot[:], quot[:], veps[:], ALU.mult).then_inc(bn_step, 1)
            dve.wait_ge(bn_step, 3)
            nc.vector.tensor_tensor(root2[:], quot[:], root[:], ALU.add).then_inc(bn_step, 1)
            dve.wait_ge(bn_step, 4)
            nc.vector.reciprocal(rinv[:], root2[:]).then_inc(bn_step, 1)
            dve.wait_ge(bn_step, 5)
            nc.vector.scalar_tensor_tensor(out=inv[:], in0=rinv[:], scalar=2.0, in1=bn[:, 0, :],
                                           op0=ALU.mult, op1=ALU.mult).then_inc(bn_step, 1)
            dve.wait_ge(bn_step, 6)
            nc.vector.tensor_tensor(mi[:], bn[:, 2, :], inv[:], ALU.mult).then_inc(bn_step, 1)
            dve.wait_ge(bn_step, 7)
            nc.vector.tensor_tensor(shift[:], bn[:, 1, :], mi[:], ALU.subtract).then_inc(bn_step, 1)
            for i in range(K):
                nc.vector.tensor_scalar(pos[:, i, :], posw[:], posh[:, i:i + 1], None,
                                        ALU.add).then_inc(bn_step, 1)
            dve.wait_ge(bn_step, 8 + K)

            with dve.Fori(0, PAIRS) as pair:
                with dve.Fori(0, QUARTERS) as u:
                    g = pair * QUARTERS + u
                    dve.wait_ge(conv_free, 6 + 3 * CHUNKS * (pair + 1))
                    for t in range(TAPS):
                        dy, dx = t // K, t % K
                        dve.wait_ge(prod_free, TAPS * g + t + 1)
                        nc.vector.scalar_tensor_tensor(
                            out=prod[:, t % 3, :].rearrange("p (a b) -> p a b", b=W),
                            in0=kp[:, bass.ds(u * QR + dy, QR), dx:dx + W],
                            scalar=pos[:, dy, dx:dx + 1],
                            in1=q[:, bass.ds(u * QT, QT)].rearrange("p (a b) -> p a b", b=W),
                            op0=ALU.add, op1=ALU.mult).then_inc(prod_ready, 1)
                    logits = ps[:, 0:3, :].rearrange("p a b -> p (a b)")[:, 0:TAPS * GP].rearrange(
                        "p (t n) -> p t n", t=TAPS)
                    dve.wait_ge(prod_free, 3 + TAPS * (g + 1))
                    nc.vector.tensor_reduce(lmax[:], logits.rearrange("p t n -> p n t"), AX_X,
                                            ALU.max).then_inc(max_ready, 1)
                    dve.wait_ge(max_ready, g + 1)
                    nc.vector.tensor_tensor(lsub[:], logits,
                                            lmax[:].rearrange("p (o n) -> p o n", o=1).broadcast_to(
                                                [P, TAPS, GP]), ALU.subtract).then_inc(sub_ready, 1)
                    dve.wait_ge(exp_ready, g + 1)
                    nc.vector.tensor_reduce(lsum[:], attn[:].rearrange("p t n -> p n t"), AX_X,
                                            ALU.add).then_inc(sum_ready, 1)
                    dve.wait_ge(sum_ready, g + 1)
                    nc.vector.reciprocal(lrcp[:], lsum[:]).then_inc(rcp_ready, 1)
                    dve.wait_ge(rcp_ready, g + 1)
                    nc.vector.tensor_tensor(attn[:], attn[:],
                                            lrcp[:].rearrange("p (o n) -> p o n", o=1).broadcast_to(
                                                [P, TAPS, GP]), ALU.mult).then_inc(attn_ready, 1)
                    dve.wait_ge(hi_ready, g + 1)
                    nc.vector.tensor_tensor(attn_lo[:], attn[:], attn_hi[:].bitcast(F32),
                                            ALU.subtract).then_inc(lo_ready, 1)
                    for hf in range(2):
                        for t in range(TAPS):
                            dy, dx = t // K, t % K
                            a = (g * 2 + hf) * TAPS + t
                            dve.wait_ge(spread_done, a + 1)
                            dve.wait_ge(av_free, a + 1)
                            nc.vector.tensor_tensor(
                                av[:, t % 3, :].rearrange("p (a b) -> p a b", b=W),
                                ps[:, 3 + (hf + t) % 2, :].rearrange("p (a b) -> p a b", b=W),
                                vp[:, bass.ds(u * QR + hf * CR + dy, CR), dx:dx + W],
                                ALU.mult).then_inc(av_ready, 1)

        @block.scalar
        def _(act):
            act.wait_ge(bn_step, 1)
            nc.scalar.activation(root[:], veps[:], ACT.Sqrt).then_inc(root_ready, 1)
            act.wait_ge(bn_step, 8)
            with act.Fori(0, PAIRS) as pair:
                act.wait_ge(av_ready, 2 + TAPS * CHUNKS * pair)
                with act.Fori(0, CHUNKS // 2) as cc:
                    for par in range(2):
                        c = cc * 2 + par
                        n = pair * CHUNKS + c
                        rows = slice(None)
                        outs = [
                            (q[:, bass.ds(c * CH, CH)].rearrange("p (a b) -> p a b", b=W), ACT.Relu, 0),
                            (kp[:, bass.ds(c * CR + 1, CR), 1:W + 1], ACT.Relu, 1),
                            (vp[:, bass.ds(c * CR + 1, CR), 1:W + 1], ACT.Identity, 2),
                        ]
                        for dst, func, j in outs:
                            act.wait_ge(conv_done, 3 * n + j + 1)
                            nc.scalar.activation(dst, ps[rows, 3 * par + j, :].rearrange(
                                "p (a b) -> p a b", b=W), func, bias=shift[:, j:j + 1],
                                scale=inv[:, j:j + 1]).then_inc(conv_free, 1)
                with act.Fori(0, QUARTERS) as u:
                    g = pair * QUARTERS + u
                    act.wait_ge(sub_ready, g + 1)
                    nc.scalar.activation(attn[:], lsub[:], ACT.Exp).then_inc(exp_ready, 1)
                    act.wait_ge(attn_ready, g + 1)
                    nc.scalar.activation(attn_hi[:], attn[:], ACT.Copy).then_inc(hi_ready, 1)
                    for hf in range(2):
                        n = g * 2 + hf
                        act.wait_ge(av_free, 3 + TAPS * (n + 1))
                        act.wait_ge(xo_free[hf], 16 * (g + 1))
                        nc.scalar.activation(xo[:, hf, :], acc[:, hf, :], ACT.Relu, bias=shift[:, 3:4],
                                             scale=inv[:, 3:4]).then_inc(xo_ready, 1)

        @block.gpsimd
        def _(pool):
            nc.gpsimd.memset(spare[:, 0:1], 0.0).then_inc(conv_free, 6)
            nc.gpsimd.memset(spare[:, 1:2], 0.0).then_inc(prod_free, 3)
            nc.gpsimd.memset(spare[:, 2:3], 0.0).then_inc(av_ready, 2)
            nc.gpsimd.memset(spare[:, 3:4], 0.0).then_inc(av_free, 3)
            nc.gpsimd.memset(spare[:, 4:5], 0.0).then_inc(xo_free[0], 16)
            nc.gpsimd.memset(spare[:, 6:7], 0.0).then_inc(xo_free[1], 16)
            nc.gpsimd.memset(spare[:, 5:6], 0.0).then_inc(xo_ready, 2)
            with pool.Fori(0, B * CHUNKS // 4) as g:
                for hf in range(2):
                    n = g * 2 + hf
                    for t in range(1, TAPS):
                        pool.wait_ge(av_ready, 2 + TAPS * n + t + 1)
                        if t == 1:
                            pool.wait_ge(xo_ready, n + 1)
                            first = av[:, 0, :]
                        else:
                            pool.wait_ge(av_free, 3 + TAPS * n + t)
                            first = acc[:, hf, :]
                        nc.gpsimd.tensor_tensor(acc[:, hf, :], first, av[:, t % 3, :], ALU.add).then_inc(
                            av_free, 2 if t == 1 else 1)

        @block.tensor
        def _(pe):
            pe.wait_ge(const_in, 16 * len(loads))
            pe.wait_ge(sel_ready, 1)
            with pe.Fori(0, PAIRS) as pair:
                pe.wait_ge(x_in, 64 * (pair + 1))
                pe.wait_ge(av_ready, 2 + TAPS * CHUNKS * pair)
                for c in range(CHUNKS):
                    y, par = c * CR, c % 2
                    pe.wait_ge(conv_free, 3 * (pair * CHUNKS + c + 1))
                    for j in range(3):
                        for i in range(2):
                            out = ps[C * i:C * i + C, 3 * par + j, :].rearrange("p (a b) -> p a b", b=W)
                            if j != 1:
                                mm = nc.tensor.matmul(out, (wq if j == 0 else wv)[:],
                                                      xp[:, i, y + 1:y + 1 + CR, 1:W + 1],
                                                      start=True, stop=True)
                                continue
                            for s in range(2 * K):
                                row = y + s // K
                                mm = nc.tensor.matmul(out, wk[:, s, :],
                                                      xp[:, i, row:row + CR, s % K:s % K + W],
                                                      start=(s == 0), stop=(s == 2 * K - 1))
                        mm.then_inc(conv_done, 1)
                with pe.Fori(0, QUARTERS) as u:
                    g = pair * QUARTERS + u
                    pe.wait_ge(conv_free, 6 + 3 * CHUNKS * (pair + 1))
                    for t in range(TAPS):
                        pe.wait_ge(prod_ready, TAPS * g + t + 1)
                        for s in range(2):
                            for j in range(4):
                                mm = nc.tensor.matmul(
                                    ps[32 * j:32 * j + 32, t // 4, (t % 4) * GP:(t % 4 + 1) * GP],
                                    headsum[:, s, :], prod[:, t % 3, (2 * j + s) * GP:(2 * j + s + 1) * GP],
                                    start=(s == 0), stop=(s == 1))
                        mm.then_inc(prod_free, 1)
                    pe.wait_ge(lo_ready, g + 1)
                    for hf in range(2):
                        for t in range(TAPS):
                            a = (g * 2 + hf) * TAPS + t
                            pe.wait_ge(av_ready, a + 1)
                            for i in range(4):
                                out = ps[:, 3 + (hf + t) % 2, i * GP:(i + 1) * GP]
                                grp = 4 * hf + i
                                nc.tensor.matmul(out, sel[:, grp, :], attn_hi[:, t, :], start=True, stop=False)
                                mm = nc.tensor.matmul(out, sel[:, grp, :], attn_lo[:, t, :], start=False, stop=True)
                            mm.then_inc(spread_done, 1)


def layer1_attention(nc, x1, consts, out):
    with ExitStack() as ctx:
        def sb(name, shape, dt=F32):
            return ctx.enter_context(nc.sbuf_tensor(name, shape, dt))

        def sem(name):
            return ctx.enter_context(nc.semaphore(name))

        KR = 3 * CI
        w_theta = sb("w_theta", [P, 2, P])
        w_phi = sb("w_phi", [P, 2, P])
        w_out = sb("w_out", [P, 2, P])
        ident = sb("ident", [P, P])
        bias = sb("bias", [P, 2])
        bw = sb("bw", [P, 1])
        spare = sb("spare1", [P, 8])
        xb = sb("xb", [P, 2, HW])
        th = sb("th", [P, 2, HW], F32R)
        ph = sb("ph", [P, 2, HW], F32R)
        th_stage = sb("th_stage", [P, CH], F32R)
        gs = sb("gs", [P, HW])
        gt = sb("gt", [P, 2, MT, 2 * CI])
        prob = sb("prob", [P, 4, 2 * CH])
        tmax = sb("tmax", [P, 4, CHUNKS])
        nmax = sb("nmax", [P, 4])
        ysb = sb("ysb", [P, CH])
        rz = sb("rz", [P, CH])
        yn = sb("yn", [P, CH])
        osb = sb("osb", [P, CH])
        ps = ctx.enter_context(nc.psum_tensor("psb", [P, 8, CH], F32))
        YB, MISC = 6, 7

        const_in = sem("const1_in")
        set_up = sem("set_up")
        gt_zeroed = sem("gt_zeroed")
        xb_in = [sem("xb_in0"), sem("xb_in1")]
        theta_mm = sem("theta_mm")
        phi_mm = sem("phi_mm")
        theta_hi = sem("theta_hi")
        phi_hi = sem("phi_hi")
        theta_lo = sem("theta_lo")
        phi_lo = sem("phi_lo")
        gt_ready = sem("gt_ready")
        staged = sem("staged")
        max_mm = sem("max_mm")
        max_free = sem("max_free")
        nmax_ready = sem("nmax_ready")
        row_mm = sem("row_mm")
        row_ready = sem("row_ready")
        score_mm = sem("score_mm")
        exp_done = sem("exp_done")
        pv_done = sem("pv_done")
        y_ready = sem("y_ready")
        out_mm = sem("out_mm")
        rz_ready = sem("rz_ready")
        yn_ready = sem("yn_ready")
        o_ready = sem("o_ready")
        o_stored = sem("o_stored")

        xb_rows = x1.rearrange("(p i) c n -> (i c) p n", i=2)
        loads = [(w_theta, "w_theta"), (w_phi, "w_phi"), (w_out, "w_out"), (ident, "ident"),
                 (bias, "bias"), (bw, "bw")]
        QUADS = B // 4

        block = ctx.enter_context(nc.Block())

        def images(eng, body, peeled=1):
            with eng.Fori(0, QUADS) as quad:
                for j in range(4):
                    b = quad * 4 + j
                    with eng.Fori(0, CHUNKS - peeled) as c:
                        body(j, c, b, False)
                    for c in range(CHUNKS - peeled, CHUNKS):
                        body(j, c, b, c == CHUNKS - 1)

        @block.sync
        def _(sp):
            for dst, name in loads:
                sp.dma_start(dst[:], consts[name]).then_inc(const_in, 16)

            def load(slot, pair):
                sp.dma_start(xb[:, slot:slot + 1, :], xb_rows[:, bass.ds(pair, 1), :]).then_inc(xb_in[slot], 16)

            def quad_stores(quad, last):
                for j in range(4):
                    with sp.Fori(0, CHUNKS) as c:
                        b = quad * 4 + j
                        r = C * (j % 2)
                        sp.wait_ge(o_ready, b * CHUNKS + c + 1)
                        sp.dma_start(out[bass.ds(b, 1), :, bass.ds(c * CH, CH)].rearrange("b c n -> c b n"),
                                     osb[r:r + C, :].rearrange("p (o n) -> p o n", o=1)).then_inc(o_stored, 16)
                    if j == 1:
                        load(0, 0 if last else quad * 2 + 2)
                    if j == 3 and not last:
                        load(1, quad * 2 + 3)

            load(0, 0)
            load(1, 1)
            with sp.Fori(0, QUADS - 1) as quad:
                quad_stores(quad, False)
            quad_stores(QUADS - 1, True)
            sp.wait_ge(o_stored, 16 + 16 * B * CHUNKS)
            sp.wait_ge(xb_in[0], 16 * (QUADS + 1))

        @block.gpsimd
        def _(pool):
            nc.gpsimd.memset(gt[:], 0.0).then_inc(gt_zeroed, 1)
            pool.wait_ge(gt_zeroed, 1)
            nc.gpsimd.memset(gt[:, :, :, CI:CI + 1], 1.0).then_inc(set_up, 1)
            nc.gpsimd.memset(spare[:, 0:1], 0.0).then_inc(max_free, 2)
            nc.gpsimd.memset(spare[:, 1:2], 0.0).then_inc(exp_done, 2)
            nc.gpsimd.memset(spare[:, 2:3], 0.0).then_inc(pv_done, 4)
            nc.gpsimd.memset(spare[:, 3:4], 0.0).then_inc(phi_lo, 1)
            nc.gpsimd.memset(spare[:, 4:5], 0.0).then_inc(y_ready, 1)
            nc.gpsimd.memset(spare[:, 5:6], 0.0).then_inc(yn_ready, 1)
            nc.gpsimd.memset(spare[:, 6:7], 0.0).then_inc(out_mm, 1)
            nc.gpsimd.memset(spare[:, 7:8], 0.0).then_inc(o_stored, 16)

        def pe_theta(n, j, c):
            return nc.tensor.matmul(ps[0:KR, MISC, :], w_theta[:, j % 2, 0:KR],
                                    xb[:, (j // 2) % 2, bass.ds(c * CH, CH)],
                                    start=True, stop=True).then_inc(theta_mm, 1)

        def pe_phi(n, j, c):
            return nc.tensor.matmul(ps[:, MISC, :], w_phi[:, j % 2, :],
                                    xb[:, (j // 2) % 2, bass.ds(c * CH, CH)],
                                    start=True, stop=True).then_inc(phi_mm, 1)

        @block.tensor
        def _(pe):
            def max_slot(k, m, buf):
                if k == 0:
                    pe.wait_ge(staged, m + 1)
                pe.wait_ge(max_free, 32 * m + k + 1)
                nc.tensor.matmul(ps[:, 4 + k % 2, :], th_stage[0:KR, (k % 4) * P:(k % 4 + 1) * P],
                                 ph[0:KR, buf, (k // 4) * CH:(k // 4 + 1) * CH],
                                 start=True, stop=True).then_inc(max_mm, 1)

            def max_row(m):
                pe.wait_ge(nmax_ready, m + 1)
                for i in range(4):
                    mm = nc.tensor.matmul(ps[KR:KR + 1, MISC, i * P:(i + 1) * P], nmax[:, i:i + 1],
                                          ident[:], start=True, stop=True)
                mm.then_inc(row_mm, 1)

            pe.wait_ge(const_in, 16 * len(loads))
            pe.wait_ge(xb_in[0], 16)
            pe.wait_ge(set_up, 2)
            with pe.Fori(0, CHUNKS) as c:
                pe.wait_ge(phi_lo, 1 + c)
                pe_theta(c, 0, c)
                pe.wait_ge(theta_lo, c + 1)
                pe_phi(c, 0, c)
            pe.wait_ge(phi_lo, 1 + CHUNKS)
            pe.wait_ge(phi_hi, 2 * CHUNKS)
            for k in range(32):
                max_slot(k, 0, 0)
            max_row(0)

            def body(j, c, b, last, quad):
                g = b * CHUNKS + c
                cur, nxt = j % 2, (j + 1) % 2
                jn = (j + 1) % 4
                mbuf = nxt if last else cur

                def weighted_sum(s):
                    pe.wait_ge(exp_done, 2 + STEPS * g + s + 1)
                    if s == 0:
                        pe.wait_ge(gt_ready, b + 1)
                        pe.wait_ge(y_ready, 1 + g)
                    for h in range(2):
                        mm = nc.tensor.matmul(ps[C * h:C * h + C, YB, :], gt[:, cur, 2 * s + h, :],
                                              prob[:, s % 4, h * CH:(h + 1) * CH],
                                              start=(s == 0), stop=(s == STEPS - 1))
                    mm.then_inc(pv_done, 1)

                pe.wait_ge(row_ready, g + 1)
                for s in range(STEPS):
                    pe.wait_ge(exp_done, STEPS * g + s + 1)
                    for h in range(2):
                        mt = 2 * s + h
                        mm = nc.tensor.matmul(ps[:, 2 * (s % 2) + h, :], ph[0:KR + 1, cur, mt * P:(mt + 1) * P],
                                              th[0:KR + 1, cur, bass.ds(c * CH, CH)], start=True, stop=True)
                    mm.then_inc(score_mm, 1)
                    if s == 2:
                        pe.wait_ge(yn_ready, 1 + g)
                        if jn == 2:
                            pe.wait_ge(xb_in[1], 16 * (quad + 1))
                        if jn == 0:
                            pe.wait_ge(xb_in[0], 16 * (quad + 2))
                        pe_theta(g, jn, c)
                    if s == 6:
                        pe.wait_ge(theta_lo, CHUNKS + g + 1)
                        pe_phi(g, jn, c)
                    for k in range(3 * s, min(3 * s + 3, 32)):
                        if last and k == 28:
                            pe.wait_ge(phi_lo, 1 + CHUNKS * (b + 2))
                        max_slot(k, g + 1, mbuf)
                    if s >= 1:
                        weighted_sum(s - 1)
                    if s == 13:
                        pe.wait_ge(phi_hi, 2 * (CHUNKS + g + 1))
                        pe.wait_ge(phi_lo, 1 + CHUNKS + g + 1)
                        max_row(g + 1)
                weighted_sum(STEPS - 1)
                pe.wait_ge(row_ready, g + 2)
                pe.wait_ge(y_ready, 1 + g + 1)
                nc.tensor.matmul(ps[:, MISC, :], w_out[:, cur, :], ysb[:], start=True, stop=True).then_inc(out_mm, 1)

            with pe.Fori(0, QUADS) as quad:
                for j in range(4):
                    b = quad * 4 + j
                    jn = (j + 1) % 4
                    with pe.Fori(0, CHUNKS - 1) as c:
                        body(j, c, b, False, quad)
                    body(j, CHUNKS - 1, b, True, quad)

        @block.scalar
        def _(act):
            def theta_upper(n, buf, c):
                act.wait_ge(theta_mm, n + 1)
                nc.scalar.activation(th[0:KR, buf, bass.ds(c * CH, CH)], ps[0:KR, MISC, :], ACT.Identity,
                                     bias=bias[0:KR, 0:1]).then_inc(theta_hi, 1)

            def phi_upper(n, buf, c, b):
                act.wait_ge(phi_mm, n + 1)
                nc.scalar.activation(ph[0:KR, buf, bass.ds(c * CH, CH)], ps[0:KR, MISC, :], ACT.Identity,
                                     bias=bias[0:KR, 1:2]).then_inc(phi_hi, 1)
                if b is not None:
                    act.wait_ge(gt_ready, b + 1)
                nc.scalar.activation(gs[KR:P, bass.ds(c * CH, CH)], ps[KR:P, MISC, :], ACT.Identity,
                                     bias=bias[KR:P, 1:2]).then_inc(phi_hi, 1)

            def row_of_maxima(m, buf, c):
                act.wait_ge(row_mm, m + 1)
                nc.scalar.activation(th[KR:KR + 1, buf, bass.ds(c * CH, CH)], ps[KR:KR + 1, MISC, :],
                                     ACT.Copy).then_inc(row_ready, 1)

            act.wait_ge(const_in, 16 * len(loads))
            with act.Fori(0, CHUNKS) as c:
                theta_upper(c, 0, c)
                phi_upper(c, 0, c, None)
            row_of_maxima(0, 0, 0)

            def body(j, c, b, last):
                g = b * CHUNKS + c
                cur, nxt = j % 2, (j + 1) % 2
                for s in range(STEPS):
                    act.wait_ge(score_mm, STEPS * g + s + 1)
                    act.wait_ge(pv_done, STEPS * g + s + 1)
                    nc.scalar.activation(prob[:, s % 4, :].rearrange("p (a b) -> p a b", a=2),
                                         ps[:, 2 * (s % 2):2 * (s % 2) + 2, :], ACT.Exp).then_inc(exp_done, 1)
                    if s == 3:
                        theta_upper(CHUNKS + g, nxt, c)
                    if s == 7:
                        phi_upper(CHUNKS + g, nxt, c, b)
                    if s == 14:
                        row_of_maxima(g + 1, nxt if last else cur, 0 if last else c + 1)
                act.wait_ge(pv_done, 4 + STEPS * (g + 1))
                act.wait_ge(out_mm, 1 + g)
                nc.scalar.copy(ysb[:], ps[:, YB, :]).then_inc(y_ready, 1)

            images(act, body)

        @block.vector
        def _(dve):
            def theta_lower(n, buf, c):
                part = th[2 * CI:KR, buf, bass.ds(c * CH, CH)]
                dve.wait_ge(theta_hi, n + 1)
                nc.vector.scalar_tensor_tensor(out=part, in0=ps[2 * CI:KR, MISC, :], scalar=bias[2 * CI:KR, 0:1],
                                               in1=part.bitcast(F32), op0=ALU.add,
                                               op1=ALU.subtract).then_inc(theta_lo, 1)

            def phi_lower(n, buf, c):
                part = ph[CI:2 * CI, buf, bass.ds(c * CH, CH)]
                dve.wait_ge(phi_hi, 2 * (n + 1))
                nc.vector.scalar_tensor_tensor(out=part, in0=ps[CI:2 * CI, MISC, :], scalar=bias[CI:2 * CI, 1:2],
                                               in1=part.bitcast(F32), op0=ALU.add,
                                               op1=ALU.subtract).then_inc(phi_lo, 1)

            def transpose_g(b, buf):
                dve.wait_ge(phi_hi, 2 * CHUNKS * (b + 1))
                for k in range(4):
                    src = gs[KR:P, :].rearrange("p (t k i) -> p t k i", k=4, i=CI)[:, :, k, :]
                    ins = nc.vector.transpose(gt[CI * k:CI * k + CI, buf, :, 0:CI], src)
                ins.then_inc(gt_ready, 1)

            def stage(have, buf, c):
                dve.wait_ge(theta_lo, have)
                nc.vector.tensor_scalar(th_stage[0:KR, :], th[0:KR, buf, bass.ds(c * CH, CH)].bitcast(F32),
                                        1.0, None, ALU.mult).then_inc(staged, 1)

            def reduce_slot(k, m):
                dve.wait_ge(max_mm, 32 * m + k + 1)
                nc.vector.tensor_reduce(tmax[:, k % 4, k // 4:k // 4 + 1], ps[:, 4 + k % 2, :], AX_X,
                                        ALU.max).then_inc(max_free, 1)

            def negated_maxima(m, first=False):
                dve.wait_ge(max_free, 2 + 32 * (m + 1))
                if not first:
                    dve.wait_ge(row_mm, m)
                nc.vector.tensor_reduce(nmax[:], tmax[:], AX_X, ALU.max, negate=True).then_inc(nmax_ready, 1)

            nc.vector.memset(ph[KR:KR + 1, :, :].bitcast(F32), 1.0).then_inc(set_up, 1)
            dve.wait_ge(const_in, 16 * len(loads))
            dve.wait_ge(set_up, 2)
            with dve.Fori(0, CHUNKS) as c:
                theta_lower(c, 0, c)
                phi_lower(c, 0, c)
            transpose_g(0, 0)
            stage(1, 0, 0)
            for k in range(32):
                reduce_slot(k, 0)
            negated_maxima(0, first=True)
            stage(2, 0, 1)

            def body(j, c, b, last):
                g = b * CHUNKS + c
                nxt = (j + 1) % 2
                for k in range(32):
                    reduce_slot(k, g + 1)
                    if k == 14:
                        theta_lower(CHUNKS + g, nxt, c)
                    if k == 26:
                        phi_lower(CHUNKS + g, nxt, c)
                negated_maxima(g + 1)
                if last or isinstance(c, int):
                    stage(CHUNKS * (b + 1) + (c + 2) % CHUNKS + 1, nxt, (c + 2) % CHUNKS)
                else:
                    stage(CHUNKS * (b + 1), j % 2, c + 2)
                if last:
                    transpose_g(b + 1, nxt)
                r = C * (j % 2)
                z = C - r
                dve.wait_ge(out_mm, 1 + g + 1)
                nc.vector.reciprocal(rz[r:r + C, :], ps[z:z + C, MISC, :]).then_inc(rz_ready, 1)
                dve.wait_ge(rz_ready, g + 1)
                nc.vector.tensor_tensor(yn[r:r + C, :], ps[r:r + C, MISC, :], rz[r:r + C, :],
                                        ALU.mult).then_inc(yn_ready, 1)
                dve.wait_ge(yn_ready, 1 + g + 1)
                dve.wait_ge(o_stored, 16 + 16 * g)
                nc.vector.scalar_tensor_tensor(out=osb[r:r + C, :], in0=yn[r:r + C, :], scalar=bw[r:r + C, :],
                                               in1=xb[r:r + C, j // 2, bass.ds(c * CH, CH)], op0=ALU.add,
                                               op1=ALU.add).then_inc(o_ready, 1)

            images(dve, body, peeled=2)


def conv_attention_kernel(nc, x, consts, out):
    x1 = nc.dram_tensor("x1_scratch", [B, C, HW], F32, kind="Internal").ap()
    layer0_attention(nc, x, consts, x1)
    layer1_attention(nc, x1, consts, out)


def lay_out(a):
    f = np.float32
    z = {}
    wk = a["L0_conv_wk"].transpose(1, 2, 3, 0)
    z["wk"] = np.zeros((P, 2 * K, C), f)
    for dx in range(K):
        z["wk"][0:C, dx] = wk[:, 0, dx]
        z["wk"][C:P, dx] = wk[:, 1, dx]
        z["wk"][C:P, K + dx] = wk[:, 2, dx]
    for n in ("q", "v"):
        z["w" + n] = np.zeros((P, C), f)
        z["w" + n][0:C] = a[f"L0_conv_w{n}"][:, :, 0, 0].T
    bn = np.stack([np.stack([a[f"L0_conv_{n}_{s}"] for n in "qkvo"], axis=-1)
                   for s in ("gamma", "beta", "mean", "var")], axis=1)
    z["bn"] = np.concatenate([bn, bn])
    z["pos_h"] = np.concatenate([a["L0_conv_pos_h"][:, :, 0]] * 2)
    z["pos_w"] = np.concatenate([a["L0_conv_pos_w"][:, 0, :]] * 2)
    z["headsum"] = np.zeros((P, 2, 32), f)
    z["sel"] = np.zeros((P, 8, P), f)
    for ch in range(P):
        head = ch // CPH
        for s in range(2):
            z["headsum"][ch, s, 16 * s + head] = 1
        for grp in range(8):
            z["sel"][16 * grp + head, grp, ch] = 1
    z["w_theta"] = np.zeros((P, 2, P), f)
    z["w_phi"] = np.zeros((P, 2, P), f)
    z["w_out"] = np.zeros((P, 2, P), f)
    for i in range(2):
        rows = slice(C * i, C * i + C)
        for r in range(3):
            z["w_theta"][rows, i, CI * r:CI * r + CI] = a["L1_conv_Wt"].T
            z["w_phi"][rows, i, CI * r:CI * r + CI] = a["L1_conv_Wp"].T
        z["w_phi"][rows, i, 3 * CI:] = a["L1_conv_Wg"].T
        for h in range(2):
            z["w_out"][C * h:C * h + CI, i, rows] = a["L1_conv_Ww"].T
            z["w_out"][C * h + CI, i, C - C * i:2 * C - C * i] = 1
    z["ident"] = np.eye(P, dtype=f)
    none = np.zeros(CI, f)
    z["bias"] = np.stack([np.concatenate([a["L1_conv_bt"]] * 3 + [none]),
                          np.concatenate([a["L1_conv_bp"]] * 3 + [a["L1_conv_bg"]])], axis=1)
    z["bw"] = np.concatenate([a["L1_conv_bw"]] * 2)[:, None]
    return z


def kernel(**inputs):
    import concourse.bacc as _bacc
    from concourse.bass_utils import run_bass_kernel_spmd as _run

    nc = _bacc.Bacc("TRN2", target_bir_lowering=False, num_devices=1)
    a = {name: np.asarray(v) for name, v in inputs.items()}
    arrays = {"x": np.ascontiguousarray(a["x"])}
    arrays.update({name: np.ascontiguousarray(v) for name, v in lay_out(a).items()})
    aps = {name: nc.dram_tensor(f"in_{name}", v.shape, mybir.dt.from_np(v.dtype), kind="ExternalInput").ap()
           for name, v in arrays.items()}
    out = nc.dram_tensor("out_0_dram", (B, C, HW), F32, kind="ExternalOutput").ap()
    conv_attention_kernel(nc, aps["x"], aps, out)
    r = _run(nc, [{f"in_{name}": v for name, v in arrays.items()}], core_ids=[0])
    return r.results[0]["out_0_dram"].reshape(B, C, H, W)
```

```python
from contextlib import ExitStack

import numpy as np

import concourse.bass as bass
from concourse import mybir

F32 = mybir.dt.float32
F16 = mybir.dt.float16
F32R = mybir.dt.float32r
ALU = mybir.AluOpType
ACT = mybir.ActivationFunctionType
AX_X = mybir.AxisListType.X

B, C, H, W = 16, 64, 64, 64
HW = H * W
K = 3
TAPS = K * K
HEADS = C // 8
CPH = C // HEADS
CI = 32
EPS = 1e-5
P = 128
PAIRS = B // 2
HP, WP = H + 2, W + 2
CH = 512
CHUNKS = HW // CH
CR = CH // W
QT = 1024
QUARTERS = HW // QT
QR = QT // W
GP = QT // 8
SPLIT = 4096.0
MT = HW // P
STEPS = MT // 2


def layer0_attention(nc, x, consts, x1):
    with ExitStack() as ctx:
        def sb(name, shape, dt=F32):
            return ctx.enter_context(nc.sbuf_tensor(name, shape, dt))

        def sem(name):
            return ctx.enter_context(nc.semaphore(name))

        wk = sb("wk", [P, 2 * K, C])
        wq = sb("wq", [P, C])
        wv = sb("wv", [P, C])
        headsum = sb("headsum", [P, 2, 32])
        sel_f = sb("sel_f", [P, 8, P])
        sel = sb("sel", [P, 8, P], F16)
        bn = sb("bn", [P, 4, 4])
        posh = sb("posh", [P, K])
        posw = sb("posw", [P, K])
        pos = sb("pos", [P, K, K])
        veps = sb("veps", [P, 4])
        root = sb("root", [P, 4])
        quot = sb("quot", [P, 4])
        root2 = sb("root2", [P, 4])
        rinv = sb("rinv", [P, 4])
        inv = sb("inv", [P, 4])
        mi = sb("mi", [P, 4])
        shift = sb("shift", [P, 4])
        spare = sb("spare", [P, 8])
        xp = sb("xp", [P, 2, HP, WP])
        kp = sb("kp", [P, HP, WP])
        vp = sb("vp", [P, HP, WP])
        q = sb("q", [P, HW])
        prod = sb("prod", [P, 3, QT])
        lmax = sb("lmax", [P, GP])
        lsub = sb("lsub", [P, TAPS, GP])
        attn = sb("attn", [P, TAPS, GP])
        lsum = sb("lsum", [P, GP])
        lrcp = sb("lrcp", [P, GP])
        attn_hi = sb("attn_hi", [P, TAPS, GP], F16)
        attn_lo = sb("attn_lo", [P, TAPS, GP], F16)
        av = sb("av", [P, 2 * TAPS, CH])
        acc = sb("acc", [P, 2, CH])
        xo = sb("xo", [P, 2, CH])
        ps = ctx.enter_context(nc.psum_tensor("psa", [P, 8, CH], F32))

        const_in = sem("const_in")
        zeroed = sem("zeroed")
        bn_step = sem("bn_step")
        root_ready = sem("root_ready")
        sel_ready = sem("sel_ready")
        x_in = sem("x_in")
        conv_done = sem("conv_done")
        conv_free = sem("conv_free")
        prod_ready = sem("prod_ready")
        prod_free = sem("prod_free")
        max_ready = sem("max_ready")
        sub_ready = sem("sub_ready")
        exp_ready = sem("exp_ready")
        sum_ready = sem("sum_ready")
        rcp_ready = sem("rcp_ready")
        attn_ready = sem("attn_ready")
        hi_ready = sem("hi_ready")
        lo_ready = sem("lo_ready")
        spread_done = sem("spread_done")
        av_ready = sem("av_ready")
        av_free = sem("av_free")
        xo_ready = sem("xo_ready")
        xo_free = [sem("xo_free0"), sem("xo_free1")]

        x_pairs = x.rearrange("(p i) c h w -> c p i h w", i=2)
        x1_rows = x1.rearrange("(p i) c n -> (i c) p n", i=2)
        loads = [(wk, "wk"), (wq, "wq"), (wv, "wv"), (headsum, "headsum"), (sel_f, "sel"),
                 (bn, "bn"), (posh, "pos_h"), (posw, "pos_w")]

        block = ctx.enter_context(nc.Block())

        @block.sync
        def _(sp):
            for dst, name in loads:
                sp.dma_start(dst[:], consts[name]).then_inc(const_in, 16)

            def load_pair(pair):
                for i in range(2):
                    src = x_pairs[:, bass.ds(pair, 1), i]
                    sp.dma_start(xp[0:C, i:i + 1, 1:H + 1, 1:W + 1], src).then_inc(x_in, 16)
                    sp.dma_start(xp[C:P, i:i + 1, 0:H, 1:W + 1], src).then_inc(x_in, 16)

            def store_pair(pair):
                with sp.Fori(0, CHUNKS // 2) as cc:
                    for par in range(2):
                        n = pair * CHUNKS + cc * 2 + par
                        sp.wait_ge(xo_ready, 2 + n + 1)
                        sp.dma_start(x1_rows[:, bass.ds(pair, 1), bass.ds((cc * 2 + par) * CH, CH)],
                                     xo[:, par:par + 1, :]).then_inc(xo_free[par], 16)

            sp.wait_ge(zeroed, 3)
            load_pair(0)
            with sp.Fori(0, PAIRS - 1) as pair:
                sp.wait_ge(conv_done, 3 * CHUNKS * (pair + 1))
                load_pair(pair + 1)
                store_pair(pair)
            store_pair(PAIRS - 1)
            for par in range(2):
                sp.wait_ge(xo_free[par], 16 + 16 * B * CHUNKS // 4)

        @block.vector
        def _(dve):
            nc.vector.memset(xp[:], 0.0).then_inc(zeroed, 1)
            nc.vector.memset(kp[:], 0.0).then_inc(zeroed, 1)
            nc.vector.memset(vp[:], 0.0).then_inc(zeroed, 1)
            dve.wait_ge(const_in, 16 * len(loads))
            nc.vector.tensor_scalar(sel[:], sel_f[:], 1.0 / SPLIT, None, ALU.mult).then_inc(sel_ready, 1)
            nc.vector.tensor_scalar(veps[:], bn[:, 3, :], EPS, None, ALU.add).then_inc(bn_step, 1)
            dve.wait_ge(root_ready, 1)
            nc.vector.reciprocal(quot[:], root[:]).then_inc(bn_step, 1)
            dve.wait_ge(bn_step, 2)
            nc.vector.tensor_tensor(quot[:], quot[:], veps[:], ALU.mult).then_inc(bn_step, 1)
            dve.wait_ge(bn_step, 3)
            nc.vector.tensor_tensor(root2[:], quot[:], root[:], ALU.add).then_inc(bn_step, 1)
            dve.wait_ge(bn_step, 4)
            nc.vector.reciprocal(rinv[:], root2[:]).then_inc(bn_step, 1)
            dve.wait_ge(bn_step, 5)
            nc.vector.scalar_tensor_tensor(out=inv[:], in0=rinv[:], scalar=2.0, in1=bn[:, 0, :],
                                           op0=ALU.mult, op1=ALU.mult).then_inc(bn_step, 1)
            dve.wait_ge(bn_step, 6)
            nc.vector.tensor_tensor(mi[:], bn[:, 2, :], inv[:], ALU.mult).then_inc(bn_step, 1)
            dve.wait_ge(bn_step, 7)
            nc.vector.tensor_tensor(shift[:], bn[:, 1, :], mi[:], ALU.subtract).then_inc(bn_step, 1)
            for i in range(K):
                nc.vector.tensor_scalar(pos[:, i, :], posw[:], posh[:, i:i + 1], None,
                                        ALU.add).then_inc(bn_step, 1)
            dve.wait_ge(bn_step, 8 + K)

            with dve.Fori(0, PAIRS) as pair:
                with dve.Fori(0, QUARTERS) as u:
                    g = pair * QUARTERS + u
                    dve.wait_ge(conv_free, 6 + 3 * CHUNKS * (pair + 1))
                    for t in range(TAPS):
                        dy, dx = t // K, t % K
                        dve.wait_ge(prod_free, TAPS * g + t + 1)
                        nc.vector.scalar_tensor_tensor(
                            out=prod[:, t % 3, :].rearrange("p (a b) -> p a b", b=W),
                            in0=kp[:, bass.ds(u * QR + dy, QR), dx:dx + W],
                            scalar=pos[:, dy, dx:dx + 1],
                            in1=q[:, bass.ds(u * QT, QT)].rearrange("p (a b) -> p a b", b=W),
                            op0=ALU.add, op1=ALU.mult).then_inc(prod_ready, 1)
                    logits = ps[:, 0:3, :].rearrange("p a b -> p (a b)")[:, 0:TAPS * GP].rearrange(
                        "p (t n) -> p t n", t=TAPS)
                    dve.wait_ge(prod_free, 3 + TAPS * (g + 1))
                    nc.vector.tensor_reduce(lmax[:], logits.rearrange("p t n -> p n t"), AX_X,
                                            ALU.max).then_inc(max_ready, 1)
                    dve.wait_ge(max_ready, g + 1)
                    nc.vector.tensor_tensor(lsub[:], logits,
                                            lmax[:].rearrange("p (o n) -> p o n", o=1).broadcast_to(
                                                [P, TAPS, GP]), ALU.subtract).then_inc(sub_ready, 1)
                    dve.wait_ge(exp_ready, g + 1)
                    nc.vector.tensor_reduce(lsum[:], attn[:].rearrange("p t n -> p n t"), AX_X,
                                            ALU.add).then_inc(sum_ready, 1)
                    dve.wait_ge(sum_ready, g + 1)
                    nc.vector.reciprocal(lrcp[:], lsum[:]).then_inc(rcp_ready, 1)
                    dve.wait_ge(rcp_ready, g + 1)
                    nc.vector.tensor_tensor(attn[:], attn[:],
                                            lrcp[:].rearrange("p (o n) -> p o n", o=1).broadcast_to(
                                                [P, TAPS, GP]), ALU.mult).then_inc(attn_ready, 1)
                    dve.wait_ge(hi_ready, g + 1)
                    nc.vector.scalar_tensor_tensor(out=attn_lo[:], in0=attn[:], scalar=SPLIT, in1=attn_hi[:],
                                                   op0=ALU.mult, op1=ALU.subtract).then_inc(lo_ready, 1)
                    for hf in range(2):
                        for t in range(TAPS):
                            dy, dx = t // K, t % K
                            a = (g * 2 + hf) * TAPS + t
                            dve.wait_ge(spread_done, a + 1)
                            dve.wait_ge(av_free, a + 1)
                            nc.vector.tensor_tensor(
                                av[:, hf * TAPS + t, :].rearrange("p (a b) -> p a b", b=W),
                                ps[:, 3 + (hf + t) % 2, :].rearrange("p (a b) -> p a b", b=W),
                                vp[:, bass.ds(u * QR + hf * CR + dy, CR), dx:dx + W],
                                ALU.mult).then_inc(av_ready, 1)

        @block.scalar
        def _(act):
            act.wait_ge(bn_step, 1)
            nc.scalar.activation(root[:], veps[:], ACT.Sqrt).then_inc(root_ready, 1)
            act.wait_ge(bn_step, 8)
            nc.scalar.activation(root[:], mi[:], ACT.Exp).then_inc(root_ready, 1)
            with act.Fori(0, PAIRS) as pair:
                act.wait_ge(av_ready, 2 + TAPS * CHUNKS * pair)
                with act.Fori(0, CHUNKS // 2) as cc:
                    for par in range(2):
                        c = cc * 2 + par
                        n = pair * CHUNKS + c
                        rows = slice(None)
                        outs = [
                            (q[:, bass.ds(c * CH, CH)].rearrange("p (a b) -> p a b", b=W), ACT.Relu, 0),
                            (kp[:, bass.ds(c * CR + 1, CR), 1:W + 1], ACT.Relu, 1),
                            (vp[:, bass.ds(c * CR + 1, CR), 1:W + 1], ACT.Identity, 2),
                        ]
                        for dst, func, j in outs:
                            act.wait_ge(conv_done, 3 * n + j + 1)
                            nc.scalar.activation(dst, ps[rows, 3 * par + j, :].rearrange(
                                "p (a b) -> p a b", b=W), func, bias=shift[:, j:j + 1],
                                scale=inv[:, j:j + 1]).then_inc(conv_free, 1)
                with act.Fori(0, QUARTERS) as u:
                    g = pair * QUARTERS + u
                    act.wait_ge(sub_ready, g + 1)
                    nc.scalar.activation(attn[:], lsub[:], ACT.Exp).then_inc(exp_ready, 1)
                    act.wait_ge(attn_ready, g + 1)
                    nc.scalar.activation(attn_hi[:], attn[:], ACT.Copy, scale=SPLIT).then_inc(hi_ready, 1)
                    for hf in range(2):
                        n = g * 2 + hf
                        act.wait_ge(av_free, 2 * TAPS + TAPS * (n + 1))
                        act.wait_ge(xo_free[hf], 16 * (g + 1))
                        nc.scalar.activation(xo[:, hf, :], acc[:, hf, :], ACT.Relu, bias=shift[:, 3:4],
                                             scale=inv[:, 3:4]).then_inc(xo_ready, 1)

        @block.gpsimd
        def _(pool):
            nc.gpsimd.memset(spare[:, 0:1], 0.0).then_inc(conv_free, 6)
            nc.gpsimd.memset(spare[:, 1:2], 0.0).then_inc(prod_free, 3)
            nc.gpsimd.memset(spare[:, 2:3], 0.0).then_inc(av_ready, 2)
            nc.gpsimd.memset(spare[:, 3:4], 0.0).then_inc(av_free, 2 * TAPS)
            nc.gpsimd.memset(spare[:, 4:5], 0.0).then_inc(xo_free[0], 16)
            nc.gpsimd.memset(spare[:, 6:7], 0.0).then_inc(xo_free[1], 16)
            nc.gpsimd.memset(spare[:, 5:6], 0.0).then_inc(xo_ready, 2)
            with pool.Fori(0, B * CHUNKS // 4) as g:
                for hf in range(2):
                    n = g * 2 + hf
                    for t in range(1, TAPS):
                        pool.wait_ge(av_ready, 2 + TAPS * n + t + 1)
                        if t == 1:
                            pool.wait_ge(xo_ready, n + 1)
                            first = av[:, hf * TAPS, :]
                        else:
                            pool.wait_ge(av_free, 2 * TAPS + TAPS * n + t)
                            first = acc[:, hf, :]
                        nc.gpsimd.tensor_tensor(acc[:, hf, :], first, av[:, hf * TAPS + t, :], ALU.add).then_inc(
                            av_free, 2 if t == 1 else 1)

        @block.tensor
        def _(pe):
            pe.wait_ge(const_in, 16 * len(loads))
            pe.wait_ge(sel_ready, 1)
            with pe.Fori(0, PAIRS) as pair:
                pe.wait_ge(x_in, 64 * (pair + 1))
                pe.wait_ge(av_ready, 2 + TAPS * CHUNKS * pair)
                for c in range(CHUNKS):
                    y, par = c * CR, c % 2
                    pe.wait_ge(conv_free, 3 * (pair * CHUNKS + c + 1))
                    for j in range(3):
                        for i in range(2):
                            out = ps[C * i:C * i + C, 3 * par + j, :].rearrange("p (a b) -> p a b", b=W)
                            if j != 1:
                                mm = nc.tensor.matmul(out, (wq if j == 0 else wv)[:],
                                                      xp[:, i, y + 1:y + 1 + CR, 1:W + 1],
                                                      start=True, stop=True)
                                continue
                            for s in range(2 * K):
                                row = y + s // K
                                mm = nc.tensor.matmul(out, wk[:, s, :],
                                                      xp[:, i, row:row + CR, s % K:s % K + W],
                                                      start=(s == 0), stop=(s == 2 * K - 1))
                        mm.then_inc(conv_done, 1)
                with pe.Fori(0, QUARTERS) as u:
                    g = pair * QUARTERS + u
                    pe.wait_ge(conv_free, 6 + 3 * CHUNKS * (pair + 1))
                    for t in range(TAPS):
                        pe.wait_ge(prod_ready, TAPS * g + t + 1)
                        for s in range(2):
                            for j in range(4):
                                mm = nc.tensor.matmul(
                                    ps[32 * j:32 * j + 32, t // 4, (t % 4) * GP:(t % 4 + 1) * GP],
                                    headsum[:, s, :], prod[:, t % 3, (2 * j + s) * GP:(2 * j + s + 1) * GP],
                                    start=(s == 0), stop=(s == 1))
                        mm.then_inc(prod_free, 1)
                    pe.wait_ge(lo_ready, g + 1)
                    for hf in range(2):
                        for t in range(TAPS):
                            a = (g * 2 + hf) * TAPS + t
                            pe.wait_ge(av_ready, a + 1)
                            for i in range(4):
                                out = ps[:, 3 + (hf + t) % 2, i * GP:(i + 1) * GP]
                                grp = 4 * hf + i
                                nc.tensor.matmul(out, sel[:, grp, :], attn_hi[:, t, :], start=True, stop=False)
                                mm = nc.tensor.matmul(out, sel[:, grp, :], attn_lo[:, t, :], start=False, stop=True)
                            mm.then_inc(spread_done, 1)


def layer1_attention(nc, x1, consts, out):
    with ExitStack() as ctx:
        def sb(name, shape, dt=F32):
            return ctx.enter_context(nc.sbuf_tensor(name, shape, dt))

        def sem(name):
            return ctx.enter_context(nc.semaphore(name))

        KR = 3 * CI
        w_theta = sb("w_theta", [P, 2, P])
        w_phi = sb("w_phi", [P, 2, P])
        w_out = sb("w_out", [P, 2, P])
        ident = sb("ident", [P, P])
        bias = sb("bias", [P, 2])
        bw = sb("bw", [P, 1])
        spare = sb("spare1", [P, 8])
        xb = sb("xb", [P, 2, HW])
        th = sb("th", [P, 2, HW], F32R)
        ph = sb("ph", [P, 2, HW], F32R)
        th_stage = sb("th_stage", [P, CH], F32R)
        gs = sb("gs", [P, HW])
        gt = sb("gt", [P, 2, MT, 2 * CI])
        prob = sb("prob", [P, 4, 2 * CH])
        tmax = sb("tmax", [P, 4, CHUNKS])
        nmax = sb("nmax", [P, 4])
        ysb = sb("ysb", [P, CH])
        rz = sb("rz", [P, CH])
        yn = sb("yn", [P, CH])
        osb = sb("osb", [P, CH])
        ps = ctx.enter_context(nc.psum_tensor("psb", [P, 8, CH], F32))
        YB, MISC = 6, 7

        const_in = sem("const1_in")
        set_up = sem("set_up")
        gt_zeroed = sem("gt_zeroed")
        xb_in = [sem("xb_in0"), sem("xb_in1")]
        theta_mm = sem("theta_mm")
        phi_mm = sem("phi_mm")
        theta_hi = sem("theta_hi")
        phi_hi = sem("phi_hi")
        theta_lo = sem("theta_lo")
        phi_lo = sem("phi_lo")
        gt_ready = sem("gt_ready")
        staged = sem("staged")
        max_mm = sem("max_mm")
        max_free = sem("max_free")
        nmax_ready = sem("nmax_ready")
        row_mm = sem("row_mm")
        row_ready = sem("row_ready")
        score_mm = sem("score_mm")
        exp_done = sem("exp_done")
        pv_done = sem("pv_done")
        y_ready = sem("y_ready")
        out_mm = sem("out_mm")
        rz_ready = sem("rz_ready")
        yn_ready = sem("yn_ready")
        o_ready = sem("o_ready")
        o_stored = sem("o_stored")

        xb_rows = x1.rearrange("(p i) c n -> (i c) p n", i=2)
        loads = [(w_theta, "w_theta"), (w_phi, "w_phi"), (w_out, "w_out"), (ident, "ident"),
                 (bias, "bias"), (bw, "bw")]
        QUADS = B // 4

        block = ctx.enter_context(nc.Block())

        MAX_SLOTS = [0] * STEPS
        for s in range(14):
            MAX_SLOTS[s] = 3 if s in (1, 8, 11, 12) else 2
        SLOT0 = [sum(MAX_SLOTS[:s]) for s in range(STEPS)]
        assert sum(MAX_SLOTS) == 32

        def images(eng, body, peeled=1):
            with eng.Fori(0, QUADS) as quad:
                for j in range(4):
                    b = quad * 4 + j
                    body(j, 0, b, quad)
                    with eng.Fori(1, CHUNKS - peeled) as c:
                        body(j, c, b, quad)
                    for c in range(CHUNKS - peeled, CHUNKS):
                        body(j, c, b, quad)

        def is_last(c):
            return isinstance(c, int) and c == CHUNKS - 1

        def is_first(c):
            return isinstance(c, int) and c == 0

        @block.sync
        def _(sp):
            for dst, name in loads:
                sp.dma_start(dst[:], consts[name]).then_inc(const_in, 16)

            def load(slot, pair):
                sp.dma_start(xb[:, slot:slot + 1, :], xb_rows[:, bass.ds(pair, 1), :]).then_inc(xb_in[slot], 16)

            def quad_stores(quad, last):
                for j in range(4):
                    with sp.Fori(0, CHUNKS) as c:
                        b = quad * 4 + j
                        r = C * (j % 2)
                        sp.wait_ge(o_ready, b * CHUNKS + c + 1)
                        sp.dma_start(out[bass.ds(b, 1), :, bass.ds(c * CH, CH)].rearrange("b c n -> c b n"),
                                     osb[r:r + C, :].rearrange("p (o n) -> p o n", o=1)).then_inc(o_stored, 16)
                    if j == 1:
                        load(0, 0 if last else quad * 2 + 2)
                    if j == 3 and not last:
                        load(1, quad * 2 + 3)

            load(0, 0)
            load(1, 1)
            with sp.Fori(0, QUADS - 1) as quad:
                quad_stores(quad, False)
            quad_stores(QUADS - 1, True)
            sp.wait_ge(o_stored, 16 + 16 * B * CHUNKS)
            sp.wait_ge(xb_in[0], 16 * (QUADS + 1))

        @block.gpsimd
        def _(pool):
            nc.gpsimd.memset(gt[:], 0.0).then_inc(gt_zeroed, 1)
            pool.wait_ge(gt_zeroed, 1)
            nc.gpsimd.memset(gt[:, :, :, CI:CI + 1], 1.0).then_inc(set_up, 1)
            nc.gpsimd.memset(spare[:, 0:1], 0.0).then_inc(max_free, 4)
            nc.gpsimd.memset(spare[:, 1:2], 0.0).then_inc(exp_done, 2)
            nc.gpsimd.memset(spare[:, 2:3], 0.0).then_inc(pv_done, 4)
            nc.gpsimd.memset(spare[:, 3:4], 0.0).then_inc(phi_lo, 1)
            nc.gpsimd.memset(spare[:, 4:5], 0.0).then_inc(y_ready, 1)
            nc.gpsimd.memset(spare[:, 5:6], 0.0).then_inc(yn_ready, 1)
            nc.gpsimd.memset(spare[:, 6:7], 0.0).then_inc(out_mm, 1)
            nc.gpsimd.memset(spare[:, 7:8], 0.0).then_inc(o_stored, 16)

        def pe_theta(n, j, c):
            return nc.tensor.matmul(ps[0:KR, MISC, :], w_theta[:, j % 2, 0:KR],
                                    xb[:, (j // 2) % 2, bass.ds(c * CH, CH)],
                                    start=True, stop=True).then_inc(theta_mm, 1)

        def pe_phi(n, j, c):
            return nc.tensor.matmul(ps[:, MISC, :], w_phi[:, j % 2, :],
                                    xb[:, (j // 2) % 2, bass.ds(c * CH, CH)],
                                    start=True, stop=True).then_inc(phi_mm, 1)

        @block.tensor
        def _(pe):
            def max_slot(k, m, buf):
                if k == 0:
                    pe.wait_ge(staged, m + 1)
                pe.wait_ge(max_free, 32 * m + k + 1)
                nc.tensor.matmul(ps[:, 2 + k % 4, :], th_stage[0:KR, (k % 4) * P:(k % 4 + 1) * P],
                                 ph[0:KR, buf, (k // 4) * CH:(k // 4 + 1) * CH],
                                 start=True, stop=True).then_inc(max_mm, 1)

            def max_row(m):
                pe.wait_ge(nmax_ready, m + 1)
                for i in range(4):
                    mm = nc.tensor.matmul(ps[KR:KR + 1, MISC, i * P:(i + 1) * P], nmax[:, i:i + 1],
                                          ident[:], start=True, stop=True)
                mm.then_inc(row_mm, 1)

            pe.wait_ge(const_in, 16 * len(loads))
            pe.wait_ge(xb_in[0], 16)
            pe.wait_ge(set_up, 2)
            with pe.Fori(0, CHUNKS) as c:
                pe.wait_ge(phi_lo, 1 + c)
                pe_theta(c, 0, c)
                pe.wait_ge(theta_lo, c + 1)
                pe_phi(c, 0, c)
            pe.wait_ge(phi_lo, 1 + CHUNKS)
            pe.wait_ge(phi_hi, 2 * CHUNKS)
            for k in range(32):
                max_slot(k, 0, 0)
            max_row(0)

            def body(j, c, b, quad):
                g = b * CHUNKS + c
                cur, nxt = j % 2, (j + 1) % 2
                jn = (j + 1) % 4
                mbuf = nxt if is_last(c) else cur

                def weighted_sum(s):
                    pe.wait_ge(exp_done, 2 + MT * g + 2 * s + 2)
                    if s == 0:
                        pe.wait_ge(gt_ready, b + 1)
                        pe.wait_ge(y_ready, 1 + g)
                    for h in range(2):
                        mm = nc.tensor.matmul(ps[C * h:C * h + C, YB, :], gt[:, cur, 2 * s + h, :],
                                              prob[:, s % 4, h * CH:(h + 1) * CH],
                                              start=(s == 0), stop=(s == STEPS - 1))
                    mm.then_inc(pv_done, 1)

                def output(done):
                    pe.wait_ge(row_ready, done + 1)
                    pe.wait_ge(y_ready, 1 + done)
                    nc.tensor.matmul(ps[:, MISC, :], w_out[:, cur, :], ysb[:], start=True,
                                     stop=True).then_inc(out_mm, 1)

                pe.wait_ge(row_ready, g + 1)
                for s in range(STEPS):
                    slots = [SLOT0[s] + i for i in range(MAX_SLOTS[s])]
                    for k in slots[:1]:
                        if is_last(c) and k >= 28:
                            pe.wait_ge(phi_lo, 1 + CHUNKS * (b + 2))
                        max_slot(k, g + 1, mbuf)
                    for h in range(2):
                        mt = 2 * s + h
                        pe.wait_ge(exp_done, MT * g + mt + 1)
                        nc.tensor.matmul(ps[:, h, :], ph[0:KR + 1, cur, mt * P:(mt + 1) * P],
                                              th[0:KR + 1, cur, bass.ds(c * CH, CH)], start=True,
                                         stop=True).then_inc(score_mm, 1)
                    if s == 1 and not is_first(c):
                        output(g)
                    if s == 6:
                        pe.wait_ge(yn_ready, 1 + g)
                        if jn == 2:
                            pe.wait_ge(xb_in[1], 16 * (quad + 1))
                        if jn == 0:
                            pe.wait_ge(xb_in[0], 16 * (quad + 2))
                        pe_theta(g, jn, c)
                    if s == 9:
                        pe.wait_ge(theta_lo, CHUNKS + g + 1)
                        pe_phi(g, jn, c)
                    for k in slots[1:2]:
                        max_slot(k, g + 1, mbuf)
                    if s == STEPS - 1:
                        pe.wait_ge(phi_hi, 2 * (CHUNKS + g + 1))
                        pe.wait_ge(phi_lo, 1 + CHUNKS + g + 1)
                        max_row(g + 1)
                    if s >= 1:
                        weighted_sum(s - 1)
                    for k in slots[2:]:
                        max_slot(k, g + 1, mbuf)
                weighted_sum(STEPS - 1)
                if is_last(c):
                    output(g + 1)

            images(pe, body)

        @block.scalar
        def _(act):
            def theta_upper(n, buf, c):
                act.wait_ge(theta_mm, n + 1)
                nc.scalar.activation(th[0:KR, buf, bass.ds(c * CH, CH)], ps[0:KR, MISC, :], ACT.Identity,
                                     bias=bias[0:KR, 0:1]).then_inc(theta_hi, 1)

            def phi_upper(n, buf, c, b):
                act.wait_ge(phi_mm, n + 1)
                nc.scalar.activation(ph[0:KR, buf, bass.ds(c * CH, CH)], ps[0:KR, MISC, :], ACT.Identity,
                                     bias=bias[0:KR, 1:2]).then_inc(phi_hi, 1)
                if b is not None:
                    act.wait_ge(gt_ready, b + 1)
                nc.scalar.activation(gs[KR:P, bass.ds(c * CH, CH)], ps[KR:P, MISC, :], ACT.Identity,
                                     bias=bias[KR:P, 1:2]).then_inc(phi_hi, 1)

            def row_of_maxima(m, buf, c):
                act.wait_ge(row_mm, m + 1)
                nc.scalar.activation(th[KR:KR + 1, buf, bass.ds(c * CH, CH)], ps[KR:KR + 1, MISC, :],
                                     ACT.Copy).then_inc(row_ready, 1)

            act.wait_ge(const_in, 16 * len(loads))
            with act.Fori(0, CHUNKS) as c:
                theta_upper(c, 0, c)
                phi_upper(c, 0, c, None)
            row_of_maxima(0, 0, 0)

            def body(j, c, b, quad):
                g = b * CHUNKS + c
                cur, nxt = j % 2, (j + 1) % 2
                for s in range(STEPS):
                    act.wait_ge(pv_done, STEPS * g + s + 1)
                    for h in range(2):
                        act.wait_ge(score_mm, MT * g + 2 * s + h + 1)
                        nc.scalar.activation(prob[:, s % 4, h * CH:(h + 1) * CH], ps[:, h, :],
                                             ACT.Exp).then_inc(exp_done, 1)
                    if s == 7:
                        theta_upper(CHUNKS + g, nxt, c)
                    if s == 10:
                        phi_upper(CHUNKS + g, nxt, c, b)
                    if s == 14:
                        if is_last(c):
                            row_of_maxima(g + 1, nxt, 0)
                        else:
                            row_of_maxima(g + 1, cur, c + 1)
                act.wait_ge(pv_done, 4 + STEPS * (g + 1))
                act.wait_ge(out_mm, 1 + g)
                nc.scalar.copy(ysb[:], ps[:, YB, :]).then_inc(y_ready, 1)

            images(act, body)

        @block.vector
        def _(dve):
            def theta_lower(n, buf, c):
                part = th[2 * CI:KR, buf, bass.ds(c * CH, CH)]
                dve.wait_ge(theta_hi, n + 1)
                nc.vector.scalar_tensor_tensor(out=part, in0=ps[2 * CI:KR, MISC, :], scalar=bias[2 * CI:KR, 0:1],
                                               in1=part.bitcast(F32), op0=ALU.add,
                                               op1=ALU.subtract).then_inc(theta_lo, 1)

            def phi_lower(n, buf, c):
                part = ph[CI:2 * CI, buf, bass.ds(c * CH, CH)]
                dve.wait_ge(phi_hi, 2 * (n + 1))
                nc.vector.scalar_tensor_tensor(out=part, in0=ps[CI:2 * CI, MISC, :], scalar=bias[CI:2 * CI, 1:2],
                                               in1=part.bitcast(F32), op0=ALU.add,
                                               op1=ALU.subtract).then_inc(phi_lo, 1)

            def transpose_g(b, buf):
                dve.wait_ge(phi_hi, 2 * CHUNKS * (b + 1))
                for k in range(4):
                    src = gs[KR:P, :].rearrange("p (t k i) -> p t k i", k=4, i=CI)[:, :, k, :]
                    ins = nc.vector.transpose(gt[CI * k:CI * k + CI, buf, :, 0:CI], src)
                ins.then_inc(gt_ready, 1)

            def stage(have, buf, c):
                dve.wait_ge(theta_lo, have)
                nc.vector.tensor_scalar(th_stage[0:KR, :], th[0:KR, buf, bass.ds(c * CH, CH)].bitcast(F32),
                                        1.0, None, ALU.mult).then_inc(staged, 1)

            def reduce_slot(k, m):
                dve.wait_ge(max_mm, 32 * m + k + 1)
                nc.vector.tensor_reduce(tmax[:, k % 4, k // 4:k // 4 + 1], ps[:, 2 + k % 4, :], AX_X,
                                        ALU.max).then_inc(max_free, 1)

            def negated_maxima(m, first=False):
                dve.wait_ge(max_free, 4 + 32 * (m + 1))
                if not first:
                    dve.wait_ge(row_mm, m)
                nc.vector.tensor_reduce(nmax[:], tmax[:], AX_X, ALU.max, negate=True).then_inc(nmax_ready, 1)

            nc.vector.memset(ph[KR:KR + 1, :, :].bitcast(F32), 1.0).then_inc(set_up, 1)
            dve.wait_ge(const_in, 16 * len(loads))
            dve.wait_ge(set_up, 2)
            with dve.Fori(0, CHUNKS) as c:
                theta_lower(c, 0, c)
                phi_lower(c, 0, c)
            transpose_g(0, 0)
            stage(1, 0, 0)
            for k in range(32):
                reduce_slot(k, 0)
            negated_maxima(0, first=True)
            stage(2, 0, 1)

            def body(j, c, b, quad):
                g = b * CHUNKS + c
                nxt = (j + 1) % 2
                r = C * (j % 2)
                z = C - r

                def reciprocals(done, part):
                    dve.wait_ge(out_mm, 1 + done)
                    cols = slice(part * P, (part + 1) * P)
                    nc.vector.reciprocal(rz[r:r + C, cols], ps[z:z + C, MISC, cols]).then_inc(rz_ready, 1)

                def normalized(done):
                    dve.wait_ge(rz_ready, 4 * done)
                    nc.vector.tensor_tensor(yn[r:r + C, :], ps[r:r + C, MISC, :], rz[r:r + C, :],
                                            ALU.mult).then_inc(yn_ready, 1)

                def finished(done, oc):
                    dve.wait_ge(yn_ready, 1 + done)
                    dve.wait_ge(o_stored, 16 * done)
                    nc.vector.scalar_tensor_tensor(out=osb[r:r + C, :], in0=yn[r:r + C, :],
                                                   scalar=bw[r:r + C, :],
                                                   in1=xb[r:r + C, j // 2, bass.ds(oc * CH, CH)],
                                                   op0=ALU.add, op1=ALU.add).then_inc(o_ready, 1)

                for s in range(STEPS):
                    for k in range(SLOT0[s], SLOT0[s] + MAX_SLOTS[s]):
                        reduce_slot(k, g + 1)
                    if not is_first(c):
                        if 2 <= s <= 5:
                            reciprocals(g, s - 2)
                        if s == 5:
                            normalized(g)
                        if s == 6:
                            finished(g, c - 1)
                    if s == 7:
                        theta_lower(CHUNKS + g, nxt, c)
                    if s == 10:
                        phi_lower(CHUNKS + g, nxt, c)
                negated_maxima(g + 1)
                if isinstance(c, int) and c >= CHUNKS - 2:
                    stage(CHUNKS * (b + 1) + (c + 2) % CHUNKS + 1, nxt, (c + 2) % CHUNKS)
                else:
                    stage(CHUNKS * (b + 1), j % 2, c + 2)
                if is_last(c):
                    transpose_g(b + 1, nxt)
                    for part in range(4):
                        reciprocals(g + 1, part)
                    normalized(g + 1)
                    finished(g + 1, c)

            images(dve, body, peeled=2)


def conv_attention_kernel(nc, x, consts, out):
    x1 = nc.dram_tensor("x1_scratch", [B, C, HW], F32, kind="Internal").ap()
    layer0_attention(nc, x, consts, x1)
    layer1_attention(nc, x1, consts, out)


def lay_out(a):
    f = np.float32
    z = {}
    wk = a["L0_conv_wk"].transpose(1, 2, 3, 0)
    z["wk"] = np.zeros((P, 2 * K, C), f)
    for dx in range(K):
        z["wk"][0:C, dx] = wk[:, 0, dx]
        z["wk"][C:P, dx] = wk[:, 1, dx]
        z["wk"][C:P, K + dx] = wk[:, 2, dx]
    for n in ("q", "v"):
        z["w" + n] = np.zeros((P, C), f)
        z["w" + n][0:C] = a[f"L0_conv_w{n}"][:, :, 0, 0].T
    bn = np.stack([np.stack([a[f"L0_conv_{n}_{s}"] for n in "qkvo"], axis=-1)
                   for s in ("gamma", "beta", "mean", "var")], axis=1)
    z["bn"] = np.concatenate([bn, bn])
    z["pos_h"] = np.concatenate([a["L0_conv_pos_h"][:, :, 0]] * 2)
    z["pos_w"] = np.concatenate([a["L0_conv_pos_w"][:, 0, :]] * 2)
    z["headsum"] = np.zeros((P, 2, 32), f)
    z["sel"] = np.zeros((P, 8, P), f)
    for ch in range(P):
        head = ch // CPH
        for s in range(2):
            z["headsum"][ch, s, 16 * s + head] = 1
        for grp in range(8):
            z["sel"][16 * grp + head, grp, ch] = 1
    z["w_theta"] = np.zeros((P, 2, P), f)
    z["w_phi"] = np.zeros((P, 2, P), f)
    z["w_out"] = np.zeros((P, 2, P), f)
    for i in range(2):
        rows = slice(C * i, C * i + C)
        for r in range(3):
            z["w_theta"][rows, i, CI * r:CI * r + CI] = a["L1_conv_Wt"].T
            z["w_phi"][rows, i, CI * r:CI * r + CI] = a["L1_conv_Wp"].T
        z["w_phi"][rows, i, 3 * CI:] = a["L1_conv_Wg"].T
        for h in range(2):
            z["w_out"][C * h:C * h + CI, i, rows] = a["L1_conv_Ww"].T
            z["w_out"][C * h + CI, i, C - C * i:2 * C - C * i] = 1
    z["ident"] = np.eye(P, dtype=f)
    none = np.zeros(CI, f)
    z["bias"] = np.stack([np.concatenate([a["L1_conv_bt"]] * 3 + [none]),
                          np.concatenate([a["L1_conv_bp"]] * 3 + [a["L1_conv_bg"]])], axis=1)
    z["bw"] = np.concatenate([a["L1_conv_bw"]] * 2)[:, None]
    return z


def kernel(**inputs):
    import concourse.bacc as _bacc
    from concourse.bass_utils import run_bass_kernel_spmd as _run

    nc = _bacc.Bacc("TRN2", target_bir_lowering=False, num_devices=1)
    a = {name: np.asarray(v) for name, v in inputs.items()}
    arrays = {"x": np.ascontiguousarray(a["x"])}
    arrays.update({name: np.ascontiguousarray(v) for name, v in lay_out(a).items()})
    aps = {name: nc.dram_tensor(f"in_{name}", v.shape, mybir.dt.from_np(v.dtype), kind="ExternalInput").ap()
           for name, v in arrays.items()}
    out = nc.dram_tensor("out_0_dram", (B, C, HW), F32, kind="ExternalOutput").ap()
    conv_attention_kernel(nc, aps["x"], aps, out)
    r = _run(nc, [{f"in_{name}": v for name, v in arrays.items()}], core_ids=[0])
    return r.results[0]["out_0_dram"].reshape(B, C, H, W)
```

```python
from contextlib import ExitStack

import numpy as np

import concourse.bass as bass
from concourse import mybir

F32 = mybir.dt.float32
F16 = mybir.dt.float16
F32R = mybir.dt.float32r
ALU = mybir.AluOpType
ACT = mybir.ActivationFunctionType
AX_X = mybir.AxisListType.X

B, C, H, W = 16, 64, 64, 64
HW = H * W
K = 3
TAPS = K * K
HEADS = C // 8
CPH = C // HEADS
CI = 32
EPS = 1e-5
P = 128
PAIRS = B // 2
HP, WP = H + 2, W + 2
CH = 512
CHUNKS = HW // CH
CR = CH // W
QT = 1024
QUARTERS = HW // QT
QR = QT // W
GP = QT // 8
SPLIT = 4096.0
AV_RING = 9
FIRST = 4
MT = HW // P
STEPS = -(-MT // 3)
SUMS = STEPS - 1
ZRING = SUMS // 2
PRING = MT // 2


def layer0_attention(nc, x, consts, x1, first, first_in):
    with ExitStack() as ctx:
        def sb(name, shape, dt=F32):
            return ctx.enter_context(nc.sbuf_tensor(name, shape, dt))

        def sem(name):
            return ctx.enter_context(nc.semaphore(name))

        wk = sb("wk", [P, 2 * K, C])
        wq = sb("wq", [P, C])
        wv = sb("wv", [P, C])
        headsum = sb("headsum", [P, 2, 32])
        sel_f = sb("sel_f", [P, 8, P])
        sel = sb("sel", [P, 8, P], F16)
        bn = sb("bn", [P, 4, 4])
        posh = sb("posh", [P, K])
        posw = sb("posw", [P, K])
        pos = sb("pos", [P, K, K])
        veps = sb("veps", [P, 4])
        root = sb("root", [P, 4])
        quot = sb("quot", [P, 4])
        root2 = sb("root2", [P, 4])
        rinv = sb("rinv", [P, 4])
        inv = sb("inv", [P, 4])
        mi = sb("mi", [P, 4])
        shift = sb("shift", [P, 4])
        spare = sb("spare", [P, 8])
        xw = sb("xw", [P, 2, 2, CR + 1, WP])
        kp = sb("kp", [P, 2, HP, WP])
        vp = sb("vp", [P, 2, HP, WP])
        q = sb("q", [P, 2, HW])
        prod = sb("prod", [P, 3, QT])
        lmax = sb("lmax", [P, GP])
        lsub = sb("lsub", [P, TAPS, GP])
        attn = sb("attn", [P, TAPS, GP])
        lsum = sb("lsum", [P, GP])
        lrcp = sb("lrcp", [P, GP])
        attn_hi = sb("attn_hi", [P, TAPS, GP], F16)
        attn_lo = sb("attn_lo", [P, TAPS, GP], F16)
        av = sb("av", [P, AV_RING, CH])
        acc = sb("acc", [P, 2, CH])
        xo = sb("xo", [P, 2, CH])
        ps = ctx.enter_context(nc.psum_tensor("psa", [P, 8, CH], F32))
        SPREAD, CONV = 2, 5

        const_in = sem("const_in")
        zeroed = sem("zeroed")
        bn_step = sem("bn_step")
        root_ready = sem("root_ready")
        sel_ready = sem("sel_ready")
        x_in = [sem("x_in0"), sem("x_in1")]
        conv_done = sem("conv_done")
        conv_free = sem("conv_free")
        prod_ready = sem("prod_ready")
        prod_free = sem("prod_free")
        max_ready = sem("max_ready")
        sub_ready = sem("sub_ready")
        exp_ready = sem("exp_ready")
        sum_ready = sem("sum_ready")
        rcp_ready = sem("rcp_ready")
        attn_ready = sem("attn_ready")
        hi_ready = sem("hi_ready")
        lo_ready = sem("lo_ready")
        spread_done = sem("spread_done")
        av_ready = sem("av_ready")
        av_free = sem("av_free")
        xo_ready = sem("xo_ready")
        xo_free = [sem("xo_free0"), sem("xo_free1")]

        x_pairs = x.rearrange("(p i) c h w -> c p i h w", i=2)
        x1_rows = x1.rearrange("(p i) c n -> (i c) p n", i=2)
        loads = [(wk, "wk"), (wq, "wq"), (wv, "wv"), (headsum, "headsum"), (sel_f, "sel"),
                 (bn, "bn"), (posh, "pos_h"), (posw, "pos_w")]

        block = ctx.enter_context(nc.Block())

        def steps(eng, step):
            with eng.Fori(0, PAIRS // 2 - 1) as d:
                for par in range(2):
                    with eng.Fori(0, QUARTERS) as u:
                        step(d * 2 + par, par, u, True)
            for par in range(2):
                with eng.Fori(0, QUARTERS) as u:
                    step(PAIRS - 2 + par, par, u, par == 0)

        @block.sync
        def _(sp):
            def load(hf, pair, c):
                for half, row in ((slice(0, C), 0), (slice(C, P), 1)):
                    sp.dma_start(xw[half, hf:hf + 1], x_pairs[:, bass.ds(pair, 1), :, bass.ds(c * CR + row, CR + 1), :])\
                        .then_inc(x_in[hf], 16)

            def load_next(n, pair, u, wrap):
                for hf in range(2):
                    sp.wait_ge(conv_done, 3 * (n + hf + 1))
                    if wrap:
                        load(hf, pair + 1, hf)
                    else:
                        load(hf, pair, 2 * u + 2 + hf)

            for dst, name in loads:
                sp.dma_start(dst[:], consts[name]).then_inc(const_in, 16)
            for hf in range(2):
                load(hf, 0, hf)
            with sp.Fori(0, QUARTERS - 1) as u:
                load_next(2 * u, 0, u, False)
            load_next(CHUNKS - 2, 0, 0, True)

            def step(pair, u, wrap, conv):
                g = pair * QUARTERS + u
                if conv:
                    load_next(CHUNKS + 2 * g, pair + 1, u, wrap)
                for hf in range(2):
                    sp.wait_ge(xo_ready, 2 + 2 * g + hf + 1)
                    sp.dma_start(x1_rows[:, bass.ds(pair, 1), bass.ds((u * 2 + hf) * CH, CH)],
                                 xo[:, hf:hf + 1, :]).then_inc(xo_free[hf], 16)

            with sp.Fori(0, PAIRS - 2) as pair:
                with sp.Fori(0, QUARTERS - 1) as u:
                    step(pair, u, False, True)
                step(pair, QUARTERS - 1, True, True)
            for name in ("w_proj", "w_out", "ident", "bias"):
                sp.dma_start(first[name][:], consts[name]).then_inc(first_in[0], 16)
            for hf in range(2):
                sp.wait_ge(xo_free[hf], 16 + 16 * QUARTERS * (PAIRS - 2))
            for pair in range(2):
                sp.dma_start(first["xb"][:, pair:pair + 1, :], x1_rows[:, pair:pair + 1, :])\
                    .then_inc(first_in[1 + pair], 16)
            with sp.Fori(0, QUARTERS - 1) as u:
                step(PAIRS - 2, u, False, True)
            step(PAIRS - 2, QUARTERS - 1, False, False)
            with sp.Fori(0, QUARTERS) as u:
                step(PAIRS - 1, u, False, False)
            for hf in range(2):
                sp.wait_ge(xo_free[hf], 16 + 16 * B * CHUNKS // 4)

        @block.vector
        def _(dve):
            nc.vector.memset(kp[:], 0.0).then_inc(zeroed, 1)
            nc.vector.memset(vp[:], 0.0).then_inc(zeroed, 1)
            dve.wait_ge(const_in, 16 * len(loads))
            nc.vector.tensor_scalar(sel[:], sel_f[:], 1.0 / SPLIT, None, ALU.mult).then_inc(sel_ready, 1)
            nc.vector.tensor_scalar(veps[:], bn[:, 3, :], EPS, None, ALU.add).then_inc(bn_step, 1)
            dve.wait_ge(root_ready, 1)
            nc.vector.reciprocal(quot[:], root[:]).then_inc(bn_step, 1)
            dve.wait_ge(bn_step, 2)
            nc.vector.tensor_tensor(quot[:], quot[:], veps[:], ALU.mult).then_inc(bn_step, 1)
            dve.wait_ge(bn_step, 3)
            nc.vector.tensor_tensor(root2[:], quot[:], root[:], ALU.add).then_inc(bn_step, 1)
            dve.wait_ge(bn_step, 4)
            nc.vector.reciprocal(rinv[:], root2[:]).then_inc(bn_step, 1)
            dve.wait_ge(bn_step, 5)
            nc.vector.scalar_tensor_tensor(out=inv[:], in0=rinv[:], scalar=2.0, in1=bn[:, 0, :],
                                           op0=ALU.mult, op1=ALU.mult).then_inc(bn_step, 1)
            dve.wait_ge(bn_step, 6)
            nc.vector.tensor_tensor(mi[:], bn[:, 2, :], inv[:], ALU.mult).then_inc(bn_step, 1)
            dve.wait_ge(bn_step, 7)
            nc.vector.tensor_tensor(shift[:], bn[:, 1, :], mi[:], ALU.subtract).then_inc(bn_step, 1)
            for i in range(K):
                nc.vector.tensor_scalar(pos[:, i, :], posw[:], posh[:, i:i + 1], None,
                                        ALU.add).then_inc(bn_step, 1)
            dve.wait_ge(bn_step, 8 + K)

            logits = ps[:, 0:3, :].rearrange("p a b -> p (a b)")[:, 0:TAPS * GP].rearrange(
                "p (t n) -> p t n", t=TAPS)
            halves = [slice(h * GP // 2, (h + 1) * GP // 2) for h in range(2)]

            def over_taps(a, h):
                return a[:, halves[h]].rearrange("p (o n) -> p o n", o=1).broadcast_to([P, TAPS, GP // 2])

            def step(pair, par, u, conv):
                g = pair * QUARTERS + u
                dve.wait_ge(conv_free, 3 + 3 * CHUNKS * (pair + 1))
                for t in range(TAPS):
                    dy, dx = t // K, t % K
                    dve.wait_ge(prod_free, TAPS * g + t + 1)
                    nc.vector.scalar_tensor_tensor(
                        out=prod[:, t % 3, :].rearrange("p (a b) -> p a b", b=W),
                        in0=kp[:, par, bass.ds(u * QR + dy, QR), dx:dx + W],
                        scalar=pos[:, dy, dx:dx + 1],
                        in1=q[:, par, bass.ds(u * QT, QT)].rearrange("p (a b) -> p a b", b=W),
                        op0=ALU.add, op1=ALU.mult).then_inc(prod_ready, 1)
                dve.wait_ge(prod_free, 3 + TAPS * (g + 1))
                for h in range(2):
                    nc.vector.tensor_reduce(lmax[:, halves[h]], logits[:, :, halves[h]].rearrange(
                        "p t n -> p n t"), AX_X, ALU.max).then_inc(max_ready, 1)
                for h in range(2):
                    dve.wait_ge(max_ready, 2 * g + h + 1)
                    nc.vector.tensor_tensor(lsub[:, :, halves[h]], logits[:, :, halves[h]],
                                            over_taps(lmax, h), ALU.subtract).then_inc(sub_ready, 1)
                for h in range(2):
                    dve.wait_ge(exp_ready, 2 * g + h + 1)
                    nc.vector.tensor_reduce(lsum[:, halves[h]], attn[:, :, halves[h]].rearrange(
                        "p t n -> p n t"), AX_X, ALU.add).then_inc(sum_ready, 1)
                for h in range(2):
                    dve.wait_ge(sum_ready, 2 * g + h + 1)
                    nc.vector.reciprocal(lrcp[:, halves[h]], lsum[:, halves[h]]).then_inc(rcp_ready, 1)
                for h in range(2):
                    dve.wait_ge(rcp_ready, 2 * g + h + 1)
                    nc.vector.tensor_tensor(attn[:, :, halves[h]], attn[:, :, halves[h]],
                                            over_taps(lrcp, h), ALU.mult).then_inc(attn_ready, 1)
                for h in range(2):
                    dve.wait_ge(hi_ready, 2 * g + h + 1)
                    nc.vector.scalar_tensor_tensor(out=attn_lo[:, :, halves[h]], in0=attn[:, :, halves[h]],
                                                   scalar=SPLIT, in1=attn_hi[:, :, halves[h]],
                                                   op0=ALU.mult, op1=ALU.subtract).then_inc(lo_ready, 1)
                for hf in range(2):
                    for t in range(TAPS):
                        dy, dx = t // K, t % K
                        a = (g * 2 + hf) * TAPS + t
                        dve.wait_ge(spread_done, a + 1)
                        dve.wait_ge(av_free, a + 1)
                        nc.vector.tensor_tensor(
                            av[:, (hf * TAPS + t) % AV_RING, :].rearrange("p (a b) -> p a b", b=W),
                            ps[:, SPREAD + t % 3, :].rearrange("p (a b) -> p a b", b=W),
                            vp[:, par, bass.ds(u * QR + hf * CR + dy, CR), dx:dx + W],
                            ALU.mult).then_inc(av_ready, 1)

            steps(dve, step)

        @block.scalar
        def _(act):
            def evacuate(n, j, par, c):
                dst = [q[:, par, bass.ds(c * CH, CH)].rearrange("p (a b) -> p a b", b=W),
                       kp[:, par, bass.ds(c * CR + 1, CR), 1:W + 1],
                       vp[:, par, bass.ds(c * CR + 1, CR), 1:W + 1]][j]
                act.wait_ge(conv_done, 3 * n + j + 1)
                nc.scalar.activation(dst, ps[:, CONV + j, :].rearrange("p (a b) -> p a b", b=W),
                                     [ACT.Relu, ACT.Relu, ACT.Identity][j], bias=shift[:, j:j + 1],
                                     scale=inv[:, j:j + 1]).then_inc(conv_free, 1)

            act.wait_ge(bn_step, 1)
            nc.scalar.activation(root[:], veps[:], ACT.Sqrt).then_inc(root_ready, 1)
            act.wait_ge(bn_step, 8)
            act.wait_ge(zeroed, 2)
            nc.scalar.activation(root[:], mi[:], ACT.Exp).then_inc(root_ready, 1)
            with act.Fori(0, QUARTERS) as u:
                for hf in range(2):
                    for j in range(3):
                        evacuate(2 * u + hf, j, 0, 2 * u + hf)

            halves = [slice(h * GP // 2, (h + 1) * GP // 2) for h in range(2)]

            def step(pair, par, u, conv):
                g = pair * QUARTERS + u

                def next_pair(hf, js):
                    if conv:
                        for j in js:
                            evacuate(CHUNKS + 2 * g + hf, j, 1 - par, 2 * u + hf)

                act.wait_ge(av_ready, 3 + TAPS * CHUNKS * pair)
                next_pair(0, [0])
                for h in range(2):
                    act.wait_ge(sub_ready, 2 * g + h + 1)
                    nc.scalar.activation(attn[:, :, halves[h]], lsub[:, :, halves[h]],
                                         ACT.Exp).then_inc(exp_ready, 1)
                next_pair(0, [1, 2])
                for h in range(2):
                    act.wait_ge(attn_ready, 2 * g + h + 1)
                    nc.scalar.activation(attn_hi[:, :, halves[h]], attn[:, :, halves[h]], ACT.Copy,
                                         scale=SPLIT).then_inc(hi_ready, 1)
                next_pair(1, [0, 1, 2])
                for hf in range(2):
                    n = g * 2 + hf
                    act.wait_ge(av_free, AV_RING + TAPS * (n + 1))
                    act.wait_ge(xo_free[hf], 16 * (g + 1))
                    nc.scalar.activation(xo[:, hf, :], acc[:, hf, :], ACT.Relu, bias=shift[:, 3:4],
                                         scale=inv[:, 3:4]).then_inc(xo_ready, 1)

            steps(act, step)

        @block.gpsimd
        def _(pool):
            for i, (s, n) in enumerate([(conv_free, 3), (prod_free, 3), (av_ready, 3), (av_free, AV_RING),
                                        (xo_free[0], 16), (xo_free[1], 16), (xo_ready, 2)]):
                nc.gpsimd.memset(spare[:, i:i + 1], 0.0).then_inc(s, n)
            with pool.Fori(0, B * CHUNKS // 4) as g:
                for hf in range(2):
                    n = g * 2 + hf
                    for t in range(1, TAPS):
                        pool.wait_ge(av_ready, 3 + TAPS * n + t + 1)
                        if t == 1:
                            pool.wait_ge(xo_ready, n + 1)
                            first = av[:, (hf * TAPS) % AV_RING, :]
                        else:
                            pool.wait_ge(av_free, AV_RING + TAPS * n + t)
                            first = acc[:, hf, :]
                        nc.gpsimd.tensor_tensor(acc[:, hf, :], first, av[:, (hf * TAPS + t) % AV_RING, :],
                                                ALU.add).then_inc(av_free, 2 if t == 1 else 1)

        @block.tensor
        def _(pe):
            PIECES = [(0, 0)] + [(1, s) for s in range(2 * K)] + [(2, 0)]

            def pieces(m, hf, which):
                for piece in which:
                    j, s = PIECES[piece]
                    if piece == 0:
                        pe.wait_ge(x_in[hf], 32 * (m + 1))
                    if s == 0:
                        pe.wait_ge(conv_free, 3 * (2 * m + hf) + j + 1)
                    row, col = (s // K, s % K) if j == 1 else (1, 1)
                    w = [wq[:], wk[:, s, :], wv[:]][j]
                    last = j != 1 or s == 2 * K - 1
                    for i in range(2):
                        mm = nc.tensor.matmul(ps[C * i:C * i + C, CONV + j, :].rearrange("p (a b) -> p a b", b=W),
                                              w, xw[:, hf, i, row:row + CR, col:col + W],
                                              start=(s == 0), stop=last)
                    if last:
                        mm.then_inc(conv_done, 1)

            pe.wait_ge(const_in, 16 * len(loads))
            pe.wait_ge(sel_ready, 1)
            with pe.Fori(0, QUARTERS) as u:
                for hf in range(2):
                    pieces(u, hf, range(8))

            def step(pair, par, u, conv):
                g = pair * QUARTERS + u
                todo = [(hf, piece) for hf in range(2) for piece in range(8)] if conv else []

                def fill(n):
                    for _ in range(min(n, len(todo))):
                        hf, piece = todo.pop(0)
                        pieces(QUARTERS + g, hf, [piece])

                for t in range(TAPS):
                    pe.wait_ge(prod_ready, TAPS * g + t + 1)
                    for s in range(2):
                        for j in range(4):
                            mm = nc.tensor.matmul(
                                ps[32 * j:32 * j + 32, t // 4, (t % 4) * GP:(t % 4 + 1) * GP],
                                headsum[:, s, :], prod[:, t % 3, (2 * j + s) * GP:(2 * j + s + 1) * GP],
                                start=(s == 0), stop=(s == 1))
                    mm.then_inc(prod_free, 1)
                    if t in (0, 1, 3, 4, 6, 7):
                        fill(1)
                fill(8)
                pe.wait_ge(lo_ready, 2 * (g + 1))
                for hf in range(2):
                    for t in range(TAPS):
                        a = (g * 2 + hf) * TAPS + t
                        pe.wait_ge(av_ready, a + 1)
                        for i in range(4):
                            out = ps[:, SPREAD + t % 3, i * GP:(i + 1) * GP]
                            grp = 4 * hf + i
                            nc.tensor.matmul(out, sel[:, grp, :], attn_hi[:, t, :], start=True, stop=False)
                            mm = nc.tensor.matmul(out, sel[:, grp, :], attn_lo[:, t, :], start=False, stop=True)
                        mm.then_inc(spread_done, 1)
                        if hf == 0 and t in (2, 6):
                            fill(1)

            steps(pe, step)


def layer1_attention(nc, x1, consts, out, first, first_in):
    with ExitStack() as ctx:
        def sb(name, shape, dt=F32):
            return ctx.enter_context(nc.sbuf_tensor(name, shape, dt))

        def sem(name):
            return ctx.enter_context(nc.semaphore(name))

        KR = 3 * CI
        w_proj, w_out, ident, bias, xb = (first[name] for name in ("w_proj", "w_out", "ident", "bias", "xb"))
        spare = sb("spare1", [P, 10])
        th = sb("th", [P, 2, HW], F32R)
        ph = sb("ph", [P, 2, HW], F32R)
        th_stage = sb("th_stage", [P, CH], F32R)
        gs = sb("gs", [P, 2, CH])
        gtc = sb("gtc", [P, 2, 4, CI])
        gt = sb("gt", [P, 2, MT, CI])
        ones = sb("ones", [P, CI])
        prob = sb("prob", [P, PRING, CH])
        psum3 = sb("psum3", [P, ZRING, CH])
        tmax = sb("tmax", [P, 4, CHUNKS])
        nmax = sb("nmax", [P, 4])
        ysb = sb("ysb", [P, CH])
        rz = sb("rz", [P, 4, 1])
        yn = sb("yn", [P, 4, C])
        osb = sb("osb", [P, CH])
        ps = ctx.enter_context(nc.psum_tensor("psb", [P, 8, CH], F32))
        YB, MISC = 6, 7

        const_in, xb_in = first_in[0], first_in[1:]
        set_up = sem("set_up")
        ones_set = sem("ones_set")
        proj_mm = sem("proj_mm")
        theta_hi = sem("theta_hi")
        phi_hi = sem("phi_hi")
        theta_lo = sem("theta_lo")
        phi_lo = sem("phi_lo")
        g_out = sem("g_out")
        transposed = sem("transposed")
        gt_ready = sem("gt_ready")
        staged = sem("staged")
        max_mm = sem("max_mm")
        max_free = sem("max_free")
        nmax_ready = sem("nmax_ready")
        row_mm = sem("row_mm")
        row_ready = sem("row_ready")
        score_mm = sem("score_mm")
        exp_done = sem("exp_done")
        pv_done = sem("pv_done")
        pair_added = sem("pair_added")
        z_ready = sem("z_ready")
        y_ready = sem("y_ready")
        out_mm = sem("out_mm")
        rz_ready = sem("rz_ready")
        yn_ready = sem("yn_ready")
        back_mm = sem("back_mm")
        o_ready = sem("o_ready")
        o_stored = sem("o_stored")

        xb_rows = x1.rearrange("(p i) c n -> (i c) p n", i=2)
        QUADS = B // 4

        block = ctx.enter_context(nc.Block())

        MAX_SLOTS = [4, 4] + [3] * (STEPS - 3) + [0]
        SLOT0 = [sum(MAX_SLOTS[:s]) for s in range(STEPS)]
        assert sum(MAX_SLOTS) == 32

        def images(eng, body, peeled=1):
            with eng.Fori(0, QUADS) as quad:
                for j in range(4):
                    b = quad * 4 + j
                    body(j, 0, b, quad)
                    with eng.Fori(1, CHUNKS - peeled) as c:
                        body(j, c, b, quad)
                    for c in range(CHUNKS - peeled, CHUNKS):
                        body(j, c, b, quad)

        def is_last(c):
            return isinstance(c, int) and c == CHUNKS - 1

        def lagging(j, c):
            if isinstance(c, int) and c == 0:
                return (j - 1, CHUNKS - 1) if j else None
            return (j, c - 1)

        @block.sync
        def _(sp):
            def load(slot, pair):
                sp.dma_start(xb[:, slot:slot + 1, :], xb_rows[:, bass.ds(pair, 1), :]).then_inc(xb_in[slot], 16)

            def quad_stores(quad, last):
                for j in range(4):
                    with sp.Fori(0, CHUNKS) as c:
                        b = quad * 4 + j
                        r = C * (j % 2)
                        sp.wait_ge(o_ready, 1 + b * CHUNKS + c + 1)
                        sp.dma_start(out[bass.ds(b, 1), :, bass.ds(c * CH, CH)].rearrange("b c n -> c b n"),
                                     osb[r:r + C, :].rearrange("p (o n) -> p o n", o=1)).then_inc(o_stored, 16)
                    if j == 1:
                        load(0, 0 if last else quad * 2 + 2)
                    if j == 3 and not last:
                        load(1, quad * 2 + 3)

            with sp.Fori(0, QUADS - 1) as quad:
                quad_stores(quad, False)
            quad_stores(QUADS - 1, True)
            sp.wait_ge(o_stored, 16 + 16 * B * CHUNKS)
            sp.wait_ge(xb_in[0], 16 * (QUADS + 1))

        @block.gpsimd
        def _(pool):
            nc.gpsimd.memset(ones[:], 0.0).then_inc(ones_set, 1)
            pool.wait_ge(ones_set, 1)
            nc.gpsimd.memset(ones[:, 0:1], 1.0).then_inc(ones_set, 1)
            pool.wait_ge(ones_set, 2)
            nc.gpsimd.memset(ph[KR:KR + 1, 1, :].bitcast(F32), 1.0).then_inc(set_up, 1)
            pool.wait_ge(set_up, 2)
            nc.gpsimd.memset(spare[:, 0:1], 0.0).then_inc(max_free, 4)
            nc.gpsimd.memset(spare[:, 1:2], 0.0).then_inc(exp_done, 2)
            nc.gpsimd.memset(spare[:, 2:3], 0.0).then_inc(pv_done, STEPS)
            nc.gpsimd.memset(spare[:, 8:9], 0.0).then_inc(z_ready, SUMS)
            nc.gpsimd.memset(spare[:, 3:4], 0.0).then_inc(phi_lo, 4)
            nc.gpsimd.memset(spare[:, 9:10], 0.0).then_inc(g_out, 4)
            nc.gpsimd.memset(spare[:, 4:5], 0.0).then_inc(y_ready, 1)
            nc.gpsimd.memset(spare[:, 5:6], 0.0).then_inc(o_ready, 1)
            nc.gpsimd.memset(spare[:, 6:7], 0.0).then_inc(out_mm, 1)
            nc.gpsimd.memset(spare[:, 7:8], 0.0).then_inc(o_stored, 16)

            def step(g, t):
                n = t // 3
                dst = psum3[:, n % ZRING, :]
                if n >= ZRING:
                    pool.wait_ge(pv_done, STEPS + STEPS * g + (n - ZRING + 1) + 1)
                else:
                    pool.wait_ge(pv_done, STEPS * g + (n + SUMS - ZRING + 1) + 1)
                pool.wait_ge(exp_done, 2 + MT * g + t + 2)
                nc.gpsimd.tensor_tensor(dst, prob[:, t % PRING, :], prob[:, (t + 1) % PRING, :],
                                        ALU.add).then_inc(pair_added, 1)
                pool.wait_ge(exp_done, 2 + MT * g + t + 3)
                pool.wait_ge(pair_added, SUMS * g + n + 1)
                nc.gpsimd.tensor_tensor(dst, dst, prob[:, (t + 2) % PRING, :], ALU.add).then_inc(z_ready, 1)

            with pool.Fori(0, B * CHUNKS) as g:
                for n in range(SUMS):
                    step(g, 3 * n)

        def pe_project(j, c, bank=MISC):
            nc.tensor.matmul(ps[:, bank, :], w_proj[:, j % 2, :], xb[:, (j // 2) % 2, bass.ds(c * CH, CH)],
                             start=True, stop=True).then_inc(proj_mm, 1)

        @block.tensor
        def _(pe):
            def max_slot(k, m, buf, projected=None):
                if k == 0:
                    pe.wait_ge(staged, m + 1)
                if projected is not None and k == 28:
                    pe.wait_ge(phi_lo, projected)
                pe.wait_ge(max_free, 32 * m + k + 1)
                nc.tensor.matmul(ps[:, 2 + k % 4, :], th_stage[0:KR, (k % 4) * P:(k % 4 + 1) * P],
                                 ph[0:KR, buf, (k // 4) * CH:(k // 4 + 1) * CH],
                                 start=True, stop=True).then_inc(max_mm, 1)

            def max_row(m):
                pe.wait_ge(nmax_ready, m + 1)
                for i in range(4):
                    mm = nc.tensor.matmul(ps[KR:KR + 1, MISC, i * P:(i + 1) * P], nmax[:, i:i + 1],
                                          ident[:], start=True, stop=True)
                mm.then_inc(row_mm, 1)

            pe.wait_ge(const_in, 16 * FIRST)
            pe.wait_ge(xb_in[0], 16)
            pe.wait_ge(set_up, 2)
            with pe.Fori(0, CHUNKS // 4) as cc:
                for par in range(4):
                    c = 4 * cc + par
                    pe.wait_ge(phi_lo, 1 + c)
                    pe.wait_ge(g_out, 1 + c)
                    pe_project(0, c, par)
            pe.wait_ge(phi_lo, 4 + CHUNKS)
            pe.wait_ge(g_out, 4 + CHUNKS)
            for k in range(32):
                max_slot(k, 0, 0)
            max_row(0)

            def body(j, c, b, quad):
                g = b * CHUNKS + c
                cur, nxt = j % 2, (j + 1) % 2
                jn = (j + 1) % 4
                mbuf = nxt if is_last(c) else cur
                projected = 4 + CHUNKS * (b + 2) if is_last(c) else None

                def weighted_sum(s):
                    tiles = range(3 * s, min(3 * s + 3, MT))
                    pe.wait_ge(exp_done, 2 + MT * g + tiles[-1] + 1)
                    if s == 0:
                        pe.wait_ge(gt_ready, CHUNKS * (b + 1))
                        pe.wait_ge(y_ready, 1 + g)
                    for t in tiles:
                        mm = nc.tensor.matmul(ps[CI * (t % 3):CI * (t % 3) + CI, YB, :], gt[:, cur, t, :],
                                              prob[:, t % PRING, :], start=(t < 3), stop=(t >= MT - 3))
                    zs = []
                    if s >= 1:
                        pe.wait_ge(z_ready, SUMS + SUMS * g + s)
                        zs.append(psum3[:, (s - 1) % ZRING, :])
                    if s == STEPS - 1:
                        zs += [prob[:, t % PRING, :] for t in tiles]
                    for i, z in enumerate(zs):
                        mm = nc.tensor.matmul(ps[KR:P, YB, :], ones[:], z, start=(s == 1),
                                              stop=(s == STEPS - 1 and i == len(zs) - 1))
                    mm.then_inc(pv_done, 1)

                def project_out(done):
                    pe.wait_ge(row_ready, done + 1)
                    pe.wait_ge(y_ready, 1 + done)
                    for i in range(4):
                        mm = nc.tensor.matmul(ps[:, MISC, i * (C + 1):(i + 1) * (C + 1)],
                                              ysb[:, i * P:(i + 1) * P], w_out[:], start=True, stop=True)
                    mm.then_inc(out_mm, 1)

                def transpose_back(done, jo):
                    pe.wait_ge(yn_ready, done)
                    r = C * (jo % 2)
                    for i in range(4):
                        mm = nc.tensor.matmul(ps[r:r + C, MISC, i * P:(i + 1) * P], yn[:, i, :], ident[:],
                                              start=True, stop=True)
                    mm.then_inc(back_mm, 1)

                lag = lagging(j, c)
                for s in range(STEPS):
                    slots = [SLOT0[s] + i for i in range(MAX_SLOTS[s])]
                    if s == 0:
                        max_slot(slots.pop(0), g + 1, mbuf, projected)
                        max_slot(slots.pop(0), g + 1, mbuf, projected)
                        pe.wait_ge(row_ready, g + 1)
                    for t in range(3 * s, min(3 * s + 3, MT)):
                        if s == 1 and t % 3 < 2:
                            max_slot(slots.pop(0), g + 1, mbuf, projected)
                        if t % 3 == 2:
                            for k in slots:
                                max_slot(k, g + 1, mbuf, projected)
                            slots = []
                        pe.wait_ge(exp_done, MT * g + t + 1)
                        nc.tensor.matmul(ps[:, t % 2, :], ph[0:KR + 1, cur, t * P:(t + 1) * P],
                                         th[0:KR + 1, cur, bass.ds(c * CH, CH)], start=True,
                                         stop=True).then_inc(score_mm, 1)
                    if s == 1 and lag:
                        project_out(g)
                    if s == 3 and lag:
                        transpose_back(g, lag[0])
                    if s == 6:
                        pe.wait_ge(o_ready, 1 + g)
                        if jn == 2:
                            pe.wait_ge(xb_in[1], 16 * (quad + 1))
                        if jn == 0:
                            pe.wait_ge(xb_in[0], 16 * (quad + 2))
                        pe_project(jn, c)
                    if s >= 1:
                        weighted_sum(s - 1)
                    if s == STEPS - 1:
                        pe.wait_ge(g_out, 4 + CHUNKS + g + 1)
                        pe.wait_ge(phi_lo, 4 + CHUNKS + g + 1)
                        max_row(g + 1)
                weighted_sum(STEPS - 1)
                if j == 3 and is_last(c):
                    project_out(g + 1)
                    transpose_back(g + 1, j)

            images(pe, body)

        @block.scalar
        def _(act):
            def theta_upper(n, buf, c, bank=MISC):
                act.wait_ge(proj_mm, n + 1)
                nc.scalar.activation(th[0:2 * CI, buf, bass.ds(c * CH, CH)], ps[0:2 * CI, bank, :],
                                     ACT.Identity, bias=bias[0:2 * CI, 0:1]).then_inc(theta_hi, 1)

            def phi_upper(rows, buf, c, bank=MISC):
                nc.scalar.activation(ph[rows, buf, bass.ds(c * CH, CH)], ps[2 * CI:KR, bank, :],
                                     ACT.Identity, bias=bias[2 * CI:KR, 1:2]).then_inc(phi_hi, 1)

            def g_whole(n, buf=0, bank=MISC, first=False):
                if not first:
                    act.wait_ge(transposed, n if bank == MISC else n - 1)
                nc.scalar.activation(gs[KR:P, buf, :], ps[KR:P, bank, :], ACT.Identity,
                                     bias=bias[KR:P, 1:2]).then_inc(g_out, 1)

            def store_g(n, gbuf, c, buf=0):
                act.wait_ge(transposed, n + 1)
                nc.scalar.copy(gt[:, gbuf, bass.ds(c * 4, 4), :], gtc[:, buf, :, :]).then_inc(gt_ready, 1)

            def row_of_maxima(m, buf, c):
                act.wait_ge(row_mm, m + 1)
                nc.scalar.activation(th[KR:KR + 1, buf, bass.ds(c * CH, CH)], ps[KR:KR + 1, MISC, :],
                                     ACT.Copy).then_inc(row_ready, 1)

            act.wait_ge(const_in, 16 * FIRST)
            for c in range(CHUNKS):
                theta_upper(c, 0, c, c % 4)
                phi_upper(slice(2 * CI, KR), 0, c, c % 4)
                phi_upper(slice(CI, 2 * CI), 0, c, c % 4)
                g_whole(c, c % 2, c % 4, first=(c < 2))
                if c:
                    store_g(c - 1, 0, c - 1, (c - 1) % 2)
            store_g(CHUNKS - 1, 0, CHUNKS - 1, 1)
            row_of_maxima(0, 0, 0)

            def body(j, c, b, quad):
                g = b * CHUNKS + c
                cur, nxt = j % 2, (j + 1) % 2
                for t in range(MT):
                    if t >= PRING:
                        act.wait_ge(pv_done, STEPS + STEPS * g + (t - PRING) // 3 + 1)
                        act.wait_ge(z_ready, SUMS + SUMS * g + (t - PRING) // 3 + 1)
                    else:
                        act.wait_ge(pv_done, STEPS * g + (t + PRING) // 3 + 1)
                        act.wait_ge(z_ready, SUMS * g + min((t + PRING) // 3 + 1, SUMS))
                    act.wait_ge(score_mm, MT * g + t + 1)
                    nc.scalar.activation(prob[:, t % PRING, :], ps[:, t % 2, :], ACT.Exp).then_inc(exp_done, 1)
                    if t == 20:
                        theta_upper(CHUNKS + g, nxt, c)
                    if t == 21:
                        phi_upper(slice(2 * CI, KR), nxt, c)
                    if t == 23:
                        phi_upper(slice(CI, 2 * CI), nxt, c)
                    if t == 24:
                        g_whole(CHUNKS + g)
                if is_last(c):
                    row_of_maxima(g + 1, nxt, 0)
                else:
                    row_of_maxima(g + 1, cur, c + 1)
                act.wait_ge(pv_done, STEPS + STEPS * (g + 1))
                act.wait_ge(out_mm, 1 + g)
                nc.scalar.copy(ysb[:], ps[:, YB, :]).then_inc(y_ready, 1)
                store_g(CHUNKS + g, nxt, c)

            images(act, body)

        @block.vector
        def _(dve):
            def theta_lower(n, buf, c, bank=MISC):
                at = bass.ds(c * CH, CH)
                dve.wait_ge(theta_hi, n + 1)
                nc.vector.scalar_tensor_tensor(out=th[2 * CI:KR, buf, at], in0=ps[0:CI, bank, :],
                                               scalar=bias[0:CI, 0:1], in1=th[0:CI, buf, at].bitcast(F32),
                                               op0=ALU.add, op1=ALU.subtract).then_inc(theta_lo, 1)

            def phi_lower(n, buf, c, bank=MISC):
                at = bass.ds(c * CH, CH)
                dve.wait_ge(phi_hi, 2 * (n + 1))
                nc.vector.scalar_tensor_tensor(out=ph[0:CI, buf, at], in0=ps[2 * CI:KR, bank, :],
                                               scalar=bias[2 * CI:KR, 1:2],
                                               in1=ph[2 * CI:KR, buf, at].bitcast(F32),
                                               op0=ALU.add, op1=ALU.subtract).then_inc(phi_lo, 1)

            def transpose_g(n, buf=0):
                dve.wait_ge(g_out, 4 + n + 1)
                if not isinstance(n, int) or n >= 2:
                    dve.wait_ge(gt_ready, n - 1 if isinstance(n, int) else n)
                for k in range(4):
                    src = gs[KR:P, buf, :].rearrange("p (t k i) -> p t k i", k=4, i=CI)[:, :, k, :]
                    ins = nc.vector.transpose(gtc[CI * k:CI * k + CI, buf, :, :], src)
                ins.then_inc(transposed, 1)

            def stage(have, buf, c):
                dve.wait_ge(theta_lo, have)
                nc.vector.tensor_scalar(th_stage[0:KR, :], th[0:KR, buf, bass.ds(c * CH, CH)].bitcast(F32),
                                        1.0, None, ALU.mult).then_inc(staged, 1)

            def reduce_slot(k, m):
                dve.wait_ge(max_mm, 32 * m + k + 1)
                nc.vector.tensor_reduce(tmax[:, k % 4, k // 4:k // 4 + 1], ps[:, 2 + k % 4, :], AX_X,
                                        ALU.max).then_inc(max_free, 1)

            def negated_maxima(m, first=False):
                dve.wait_ge(max_free, 4 + 32 * (m + 1))
                if not first:
                    dve.wait_ge(row_mm, m)
                nc.vector.tensor_reduce(nmax[:], tmax[:], AX_X, ALU.max, negate=True).then_inc(nmax_ready, 1)

            nc.vector.memset(ph[KR:KR + 1, 0, :].bitcast(F32), 1.0).then_inc(set_up, 1)
            dve.wait_ge(const_in, 16 * FIRST)
            dve.wait_ge(set_up, 2)
            for c in range(CHUNKS):
                theta_lower(c, 0, c, c % 4)
                phi_lower(c, 0, c, c % 4)
                transpose_g(c, c % 2)
            stage(1, 0, 0)
            for k in range(32):
                reduce_slot(k, 0)
            negated_maxima(0, first=True)
            stage(2, 0, 1)

            def body(j, c, b, quad):
                g = b * CHUNKS + c
                nxt = (j + 1) % 2
                def normalize(done):
                    dve.wait_ge(out_mm, 1 + done)
                    both = ps[:, MISC, 0:4 * (C + 1)].rearrange("p (i n) -> p i n", i=4)
                    nc.vector.reciprocal(rz[:], both[:, :, C:C + 1]).then_inc(rz_ready, 1)
                    dve.wait_ge(rz_ready, done)
                    nc.vector.tensor_tensor(yn[:], both[:, :, 0:C], rz[:].broadcast_to([P, 4, C]),
                                            ALU.mult).then_inc(yn_ready, 1)

                def add_x1(done, jo, co):
                    r = C * (jo % 2)
                    dve.wait_ge(back_mm, done)
                    dve.wait_ge(o_stored, 16 * done)
                    nc.vector.tensor_tensor(osb[r:r + C, :], ps[r:r + C, MISC, :],
                                            xb[r:r + C, jo // 2, bass.ds(co * CH, CH)],
                                            ALU.add).then_inc(o_ready, 1)

                lag = lagging(j, c)
                for s in range(STEPS):
                    for k in range(SLOT0[s], SLOT0[s] + MAX_SLOTS[s]):
                        if k == 26:
                            theta_lower(CHUNKS + g, nxt, c)
                        if k == 28:
                            phi_lower(CHUNKS + g, nxt, c)
                        if k == 30:
                            transpose_g(CHUNKS + g)
                        reduce_slot(k, g + 1)
                    if s == 2 and lag:
                        normalize(g)
                    if s == 4 and lag:
                        add_x1(g, *lag)
                negated_maxima(g + 1)
                if isinstance(c, int) and c >= CHUNKS - 2:
                    stage(CHUNKS * (b + 1) + (c + 2) % CHUNKS + 1, nxt, (c + 2) % CHUNKS)
                else:
                    stage(CHUNKS * (b + 1), j % 2, c + 2)
                if j == 3 and is_last(c):
                    normalize(g + 1)
                    add_x1(g + 1, j, c)

            images(dve, body, peeled=2)


def conv_attention_kernel(nc, x, consts, out):
    x1 = nc.dram_tensor("x1_scratch", [B, C, HW], F32, kind="Internal").ap()
    with ExitStack() as ctx:
        first = {name: ctx.enter_context(nc.sbuf_tensor(name, shape, F32)) for name, shape in
                 (("w_proj", [P, 2, P]), ("w_out", [P, C + 1]), ("ident", [P, P]), ("bias", [P, 2]),
                  ("xb", [P, 2, HW]))}
        first_in = [ctx.enter_context(nc.semaphore(name)) for name in ("const1_in", "xb_in0", "xb_in1")]
        layer0_attention(nc, x, consts, x1, first, first_in)
        layer1_attention(nc, x1, consts, out, first, first_in)


def lay_out(a):
    f = np.float32
    z = {}
    wk = a["L0_conv_wk"].transpose(1, 2, 3, 0)
    z["wk"] = np.zeros((P, 2 * K, C), f)
    for dx in range(K):
        z["wk"][0:C, dx] = wk[:, 0, dx]
        z["wk"][C:P, dx] = wk[:, 1, dx]
        z["wk"][C:P, K + dx] = wk[:, 2, dx]
    for n in ("q", "v"):
        z["w" + n] = np.zeros((P, C), f)
        z["w" + n][0:C] = a[f"L0_conv_w{n}"][:, :, 0, 0].T
    bn = np.stack([np.stack([a[f"L0_conv_{n}_{s}"] for n in "qkvo"], axis=-1)
                   for s in ("gamma", "beta", "mean", "var")], axis=1)
    z["bn"] = np.concatenate([bn, bn])
    z["pos_h"] = np.concatenate([a["L0_conv_pos_h"][:, :, 0]] * 2)
    z["pos_w"] = np.concatenate([a["L0_conv_pos_w"][:, 0, :]] * 2)
    z["headsum"] = np.zeros((P, 2, 32), f)
    z["sel"] = np.zeros((P, 8, P), f)
    for ch in range(P):
        head = ch // CPH
        for s in range(2):
            z["headsum"][ch, s, 16 * s + head] = 1
        for grp in range(8):
            z["sel"][16 * grp + head, grp, ch] = 1
    z["w_proj"] = np.zeros((P, 2, P), f)
    z["w_out"] = np.zeros((P, C + 1), f)
    z["w_out"][0:3 * CI, 0:C] = np.concatenate([a["L1_conv_Ww"].T] * 3)
    z["w_out"][3 * CI, 0:C] = a["L1_conv_bw"]
    z["w_out"][3 * CI, C] = 1
    for i in range(2):
        rows = slice(C * i, C * i + C)
        z["w_proj"][rows, i] = np.concatenate([a[f"L1_conv_W{n}"].T for n in "ttpg"], axis=1)
    z["ident"] = np.eye(P, dtype=f)
    none = np.zeros(CI, f)
    z["bias"] = np.stack([np.concatenate([a["L1_conv_bt"]] * 3 + [none]),
                          np.concatenate([a["L1_conv_bp"]] * 3 + [a["L1_conv_bg"]])], axis=1)
    return z


def kernel(**inputs):
    import concourse.bacc as _bacc
    from concourse.bass_utils import run_bass_kernel_spmd as _run

    nc = _bacc.Bacc("TRN2", target_bir_lowering=False, num_devices=1)
    a = {name: np.asarray(v) for name, v in inputs.items()}
    x = np.zeros((B, C, HP, WP), np.float32)
    x[:, :, 1:H + 1, 1:W + 1] = a["x"]
    arrays = {"x": x}
    arrays.update({name: np.ascontiguousarray(v) for name, v in lay_out(a).items()})
    aps = {name: nc.dram_tensor(f"in_{name}", v.shape, mybir.dt.from_np(v.dtype), kind="ExternalInput").ap()
           for name, v in arrays.items()}
    out = nc.dram_tensor("out_0_dram", (B, C, HW), F32, kind="ExternalOutput").ap()
    conv_attention_kernel(nc, aps["x"], aps, out)
    r = _run(nc, [{f"in_{name}": v for name, v in arrays.items()}], core_ids=[0])
    return r.results[0]["out_0_dram"].reshape(B, C, H, W)
```
